# Optimizing a Trainium2 kernel written in Bass

```python
import numpy as np
import jax
import jax.numpy as jnp

def _softmax(x, axis=-1):
    return jax.nn.softmax(x, axis=axis)

def _gelu(x):
    return jax.nn.gelu(x, approximate=True)

def _silu(x):
    return jax.nn.silu(x)

def _sigmoid(x):
    return jax.nn.sigmoid(x)

def _layernorm(x, axis=-1, eps=1e-05):
    m = jnp.mean(x, axis=axis, keepdims=True)
    v = jnp.var(x, axis=axis, keepdims=True)
    return (x - m) / jnp.sqrt(v + eps)

def _scatter_add(tgt, idx, src, axis=0):
    return tgt.at[idx].add(src)

def _segment_sum(src, seg, n):
    return jax.ops.segment_sum(src, seg, n)
kernel_name = 'mk_adj_resnorm_d2_adj_r2_90cfc2'

def setup_inputs(seed: int=0):
    np.random.seed(seed)
    _w = jnp.asarray

    def _rec_inputs():
        import jax
        import jax.numpy as jnp
        _gk = jax.random.key(seed)
        x = -0.0005207 + 1.001 * jax.random.normal(jax.random.fold_in(_gk, 1), (4096, 128), jnp.float32)
        _a = jax.random.bernoulli(jax.random.fold_in(_gk, 2), 0.00390625, (4096, 4096))
        _a = jnp.logical_or(_a, jnp.swapaxes(_a, -1, -2))
        _a = jnp.logical_or(_a, jnp.eye(4096, dtype=bool))
        _af = _a.astype(jnp.float32)
        _af = _af * jax.random.uniform(jax.random.fold_in(_gk, 3), (4096, 4096), jnp.float32, 0.05, 1)
        adj = _af
        return (x, adj)
    x, adj = _rec_inputs()

    def _L0_gnn_setup():
        import jax, jax.numpy as jnp
        import numpy as np
        N = 4096
        D = 128
        L = 3

        def _cxin_conv(x, a, eps, W, b):
            ax = a @ x
            h = ax + (1.0 + eps[0]) * ax
            for i in range(L):
                h = jax.nn.relu(h @ W[i].T + b[i])
            return h
        key = jax.random.key(seed)
        ks = jax.random.split(key, 8)
        s = 1.0 / np.sqrt(D)
        return {'x1': jax.random.normal(ks[0], (N, D), jnp.float32), 'x2': jax.random.normal(ks[1], (N, D), jnp.float32), 'G1': jax.random.uniform(ks[2], (N, N), jnp.float32), 'G2': jax.random.uniform(ks[3], (N, N), jnp.float32), 'eps1': jnp.zeros((1,), jnp.float32), 'eps2': jnp.zeros((1,), jnp.float32), 'W1': jax.random.normal(ks[4], (L, D, D), jnp.float32) * s, 'b1': jnp.zeros((L, D), jnp.float32), 'W2': jax.random.normal(ks[5], (L, D, D), jnp.float32) * s, 'b2': jnp.zeros((L, D), jnp.float32), 'Wm': jax.random.normal(ks[6], (D, 2 * D), jnp.float32) * (1.0 / np.sqrt(2 * D)), 'bm': jnp.zeros((D,), jnp.float32)}
    _L0_gnn_all = _L0_gnn_setup()
    _L0_gnn_in = {k: v for k, v in _L0_gnn_all.items() if k in ('x2', 'eps1', 'eps2', 'W1', 'b1', 'W2', 'b2', 'Wm', 'bm')}
    del _L0_gnn_all

    def _L1_gnn_setup():
        import jax, jax.numpy as jnp
        import numpy as np
        from jax import lax
        D_MODEL = 128
        D_STATE = 16
        D_CONV = 4
        EXPAND = 2
        D_INNER = EXPAND * D_MODEL
        DT_RANK = (D_MODEL + 15) // 16
        N = 2048
        EPS = 1e-05

        def _mamba(h, w_in, conv_w, conv_b, w_xp, w_dt, b_dt, A_log, D_skip, w_out):
            L = h.shape[0]
            xz = h @ w_in
            xc, z = (xz[:, :D_INNER], xz[:, D_INNER:])
            xpad = jnp.pad(xc, ((D_CONV - 1, 0), (0, 0)))
            xconv = sum((xpad[k:k + L] * conv_w[:, k] for k in range(D_CONV))) + conv_b
            u = jax.nn.silu(xconv)
            dbc = u @ w_xp
            dt = jax.nn.softplus(dbc[:, :DT_RANK] @ w_dt + b_dt)
            B = dbc[:, DT_RANK:DT_RANK + D_STATE]
            C = dbc[:, DT_RANK + D_STATE:]
            A = -jnp.exp(A_log)
            dA = jnp.exp(dt[:, :, None] * A[None])
            dBu = dt[:, :, None] * B[:, None, :] * u[:, :, None]

            def step(hst, inp):
                dAt, dBut, Ct = inp
                hst = dAt * hst + dBut
                return (hst, hst @ Ct)
            _, ys = lax.scan(step, jnp.zeros((D_INNER, D_STATE), h.dtype), (dA, dBu, C))
            y = ys + u * D_skip
            y = y * jax.nn.silu(z)
            return y @ w_out
        key = jax.random.key(seed)
        ks = jax.random.split(key, 16)
        x = jax.random.normal(ks[0], (N, D_MODEL), dtype=jnp.float32)
        a = jax.random.uniform(ks[1], (N, N), dtype=jnp.float32)
        adj = a / a.sum(axis=1, keepdims=True)
        s = lambda fi, fo: 1.0 / np.sqrt(fi)
        gcn_w = jax.random.uniform(ks[2], (D_MODEL, D_MODEL), jnp.float32, -s(D_MODEL, 0), s(D_MODEL, 0))
        gcn_b = jnp.zeros((D_MODEL,), jnp.float32)
        ln_g = jnp.ones((D_MODEL,), jnp.float32)
        ln_b = jnp.zeros((D_MODEL,), jnp.float32)
        w_in = jax.random.normal(ks[3], (D_MODEL, 2 * D_INNER), jnp.float32) * s(D_MODEL, 0)
        conv_w = jax.random.normal(ks[4], (D_INNER, D_CONV), jnp.float32) * s(D_CONV, 0)
        conv_b = jnp.zeros((D_INNER,), jnp.float32)
        w_xp = jax.random.normal(ks[5], (D_INNER, DT_RANK + 2 * D_STATE), jnp.float32) * s(D_INNER, 0)
        w_dt = jax.random.normal(ks[6], (DT_RANK, D_INNER), jnp.float32) * s(DT_RANK, 0)
        b_dt = jnp.log(jnp.expm1(jnp.exp(jax.random.uniform(ks[7], (D_INNER,), jnp.float32, np.log(0.001), np.log(0.1)))))
        A_log = jnp.log(jnp.broadcast_to(jnp.arange(1, D_STATE + 1, dtype=jnp.float32), (D_INNER, D_STATE)))
        D_skip = jnp.ones((D_INNER,), jnp.float32)
        w_out = jax.random.normal(ks[8], (D_INNER, D_MODEL), jnp.float32) * s(D_INNER, 0)
        return dict(x=x, adj=adj, gcn_w=gcn_w, gcn_b=gcn_b, ln_g=ln_g, ln_b=ln_b, w_in=w_in, conv_w=conv_w, conv_b=conv_b, w_xp=w_xp, w_dt=w_dt, b_dt=b_dt, A_log=A_log, D_skip=D_skip, w_out=w_out)
    _L1_gnn_all = _L1_gnn_setup()
    _L1_gnn_in = {k: v for k, v in _L1_gnn_all.items() if k in ('gcn_w', 'gcn_b', 'ln_g', 'ln_b', 'w_in', 'conv_w', 'conv_b', 'w_xp', 'w_dt', 'b_dt', 'A_log', 'D_skip', 'w_out')}
    del _L1_gnn_all
    return {'x': x, 'adj': adj, 'L0_gnn_x2': _L0_gnn_in['x2'], 'L0_gnn_eps1': _L0_gnn_in['eps1'], 'L0_gnn_eps2': _L0_gnn_in['eps2'], 'L0_gnn_W1': _L0_gnn_in['W1'], 'L0_gnn_b1': _L0_gnn_in['b1'], 'L0_gnn_W2': _L0_gnn_in['W2'], 'L0_gnn_b2': _L0_gnn_in['b2'], 'L0_gnn_Wm': _L0_gnn_in['Wm'], 'L0_gnn_bm': _L0_gnn_in['bm'], 'L1_gnn_gcn_w': _L1_gnn_in['gcn_w'], 'L1_gnn_gcn_b': _L1_gnn_in['gcn_b'], 'L1_gnn_ln_g': _L1_gnn_in['ln_g'], 'L1_gnn_ln_b': _L1_gnn_in['ln_b'], 'L1_gnn_w_in': _L1_gnn_in['w_in'], 'L1_gnn_conv_w': _L1_gnn_in['conv_w'], 'L1_gnn_conv_b': _L1_gnn_in['conv_b'], 'L1_gnn_w_xp': _L1_gnn_in['w_xp'], 'L1_gnn_w_dt': _L1_gnn_in['w_dt'], 'L1_gnn_b_dt': _L1_gnn_in['b_dt'], 'L1_gnn_A_log': _L1_gnn_in['A_log'], 'L1_gnn_D_skip': _L1_gnn_in['D_skip'], 'L1_gnn_w_out': _L1_gnn_in['w_out']}

def reference(x, adj, L0_gnn_x2, L0_gnn_eps1, L0_gnn_eps2, L0_gnn_W1, L0_gnn_b1, L0_gnn_W2, L0_gnn_b2, L0_gnn_Wm, L0_gnn_bm, L1_gnn_gcn_w, L1_gnn_gcn_b, L1_gnn_ln_g, L1_gnn_ln_b, L1_gnn_w_in, L1_gnn_conv_w, L1_gnn_conv_b, L1_gnn_w_xp, L1_gnn_w_dt, L1_gnn_b_dt, L1_gnn_A_log, L1_gnn_D_skip, L1_gnn_w_out):
    import jax
    import jax.numpy as jnp

    def _L0_gnn_ref(x1, x2, G1, G2, eps1, eps2, W1, b1, W2, b2, Wm, bm):
        import jax, jax.numpy as jnp
        import numpy as np
        N = 4096
        D = 128
        L = 3

        def _cxin_conv(x, a, eps, W, b):
            ax = a @ x
            h = ax + (1.0 + eps[0]) * ax
            for i in range(L):
                h = jax.nn.relu(h @ W[i].T + b[i])
            return h
        out1 = _cxin_conv(x1, G1, eps1, W1, b1)
        out2 = _cxin_conv(x2, G2, eps2, W2, b2)
        merged = jnp.concatenate((out1, out2), axis=1)
        return merged @ Wm.T + bm

    def _L1_gnn_ref(x, adj, gcn_w, gcn_b, ln_g, ln_b, w_in, conv_w, conv_b, w_xp, w_dt, b_dt, A_log, D_skip, w_out):
        import jax, jax.numpy as jnp
        import numpy as np
        from jax import lax
        D_MODEL = 128
        D_STATE = 16
        D_CONV = 4
        EXPAND = 2
        D_INNER = EXPAND * D_MODEL
        DT_RANK = (D_MODEL + 15) // 16
        N = 2048
        EPS = 1e-05

        def _mamba(h, w_in, conv_w, conv_b, w_xp, w_dt, b_dt, A_log, D_skip, w_out):
            L = h.shape[0]
            xz = h @ w_in
            xc, z = (xz[:, :D_INNER], xz[:, D_INNER:])
            xpad = jnp.pad(xc, ((D_CONV - 1, 0), (0, 0)))
            xconv = sum((xpad[k:k + L] * conv_w[:, k] for k in range(D_CONV))) + conv_b
            u = jax.nn.silu(xconv)
            dbc = u @ w_xp
            dt = jax.nn.softplus(dbc[:, :DT_RANK] @ w_dt + b_dt)
            B = dbc[:, DT_RANK:DT_RANK + D_STATE]
            C = dbc[:, DT_RANK + D_STATE:]
            A = -jnp.exp(A_log)
            dA = jnp.exp(dt[:, :, None] * A[None])
            dBu = dt[:, :, None] * B[:, None, :] * u[:, :, None]

            def step(hst, inp):
                dAt, dBut, Ct = inp
                hst = dAt * hst + dBut
                return (hst, hst @ Ct)
            _, ys = lax.scan(step, jnp.zeros((D_INNER, D_STATE), h.dtype), (dA, dBu, C))
            y = ys + u * D_skip
            y = y * jax.nn.silu(z)
            return y @ w_out
        h = jax.nn.relu(adj @ x @ gcn_w + gcn_b)
        mu = h.mean(-1, keepdims=True)
        var = h.var(-1, keepdims=True)
        h = (h - mu) * lax.rsqrt(var + EPS) * ln_g + ln_b
        return _mamba(h, w_in, conv_w, conv_b, w_xp, w_dt, b_dt, A_log, D_skip, w_out)
    x = _layernorm(x + _L0_gnn_ref(x, L0_gnn_x2, adj, adj, L0_gnn_eps1, L0_gnn_eps2, L0_gnn_W1, L0_gnn_b1, L0_gnn_W2, L0_gnn_b2, L0_gnn_Wm, L0_gnn_bm), axis=-1)
    x = _layernorm(x + _L1_gnn_ref(x, adj, L1_gnn_gcn_w, L1_gnn_gcn_b, L1_gnn_ln_g, L1_gnn_ln_b, L1_gnn_w_in, L1_gnn_conv_w, L1_gnn_conv_b, L1_gnn_w_xp, L1_gnn_w_dt, L1_gnn_b_dt, L1_gnn_A_log, L1_gnn_D_skip, L1_gnn_w_out), axis=-1)
    return x

_drawn_inputs = setup_inputs


def setup_inputs(seed=0):
    import zlib

    import numpy as np

    out = dict(_drawn_inputs(seed))
    spreads = {'L0_gnn_b1': (0.0, 0.294),
     'L0_gnn_b2': (0.0, 0.311),
     'L0_gnn_bm': (0.0, 0.1),
     'L1_gnn_gcn_b': (0.0, 0.785),
     'L1_gnn_ln_g': (1.0, 0.2),
     'L1_gnn_ln_b': (0.0, 0.1),
     'L1_gnn_conv_b': (0.0, 0.288),
     'L1_gnn_D_skip': (1.0, 0.2)}
    factors = {'L1_gnn_w_dt': 3.777}
    for name, (base, spread) in spreads.items():
        noise = np.random.default_rng([zlib.crc32(name.encode()), seed]).standard_normal(out[name].shape)
        drawn = base * np.exp(spread * noise) if base else spread * noise
        out[name] = jnp.asarray(drawn.astype(out[name].dtype))
    for name, factor in factors.items():
        out[name] = (out[name] * factor).astype(out[name].dtype)
    return out
```

```python
from contextlib import ExitStack

import concourse.bass as bass
from concourse import mybir

F32 = mybir.dt.float32
F32R = mybir.dt.float32r
ALU = mybir.AluOpType
ACT = mybir.ActivationFunctionType

P = 128
N = 4096
D = 128
TILE = 512
TILES = N // TILE
KB = N // P
CH = 4
CHUNKS = KB // CH
CHC = CH * TILE
Q = 4
GROUPS = TILE // 32
PIECES = 4
PC = N // Q // PIECES
RG = TILE // P
LAYERS = 3
DI = 256
H = 2
S = 16
R = 8
TAPS = 4
EPS = 1e-5


def wait(eng, sem, value):
    if not isinstance(value, int) or value > 0:
        eng.wait_ge(sem, value)


def gnn_mamba(nc, x, adj, x2, eps1, eps2, W1, b1, W2, b2, Wm, bm, gcn_w, gcn_b, ln_g, ln_b, w_in, conv_w,
              conv_b, w_xp, w_dt, b_dt, A_log, D_skip, w_out, out, POOL_B=(2, 5, 8, 11, 14)):
    ctx = ExitStack()
    with ctx:
        def sem(name):
            return ctx.enter_context(nc.semaphore(name))

        def sb(name, shape, dt=F32, stack=ctx):
            return stack.enter_context(nc.sbuf_tensor(name, shape, dt))

        adjT = nc.dram_tensor("adjT", (TILES * CHUNKS * P, CHC), F32, kind="Internal").ap()
        mid = nc.dram_tensor("mid", (N, D), F32, kind="Internal").ap()

        ident = sb("ident", [P, P])
        neg_half = sb("neg_half", [P, RG])
        eps_ln = sb("eps_ln", [P, RG])
        gcn_w_sb = sb("gcn_w_sb", [P, D])
        gcn_b_sb = sb("gcn_b_sb", [P, D])
        bm_sb = sb("bm_sb", [P, D])
        ln_g_sb = sb("ln_g_sb", [P, 1])
        ln_b_sb = sb("ln_b_sb", [P, 1])
        w_in_sb = sb("w_in_sb", [P, 2 * DI])
        conv_w_sb = sb("conv_w_sb", [P, H, TAPS])
        conv_b_sb = sb("conv_b_sb", [P, H])
        w_xp_sb = sb("w_xp_sb", [P, H, 2 * 2 * S + R])
        w_dt_sb = sb("w_dt_sb", [P, DI])
        b_dt_sb = sb("b_dt_sb", [P, H])
        A_sb = sb("A_sb", [P, H, S])
        D_sb = sb("D_sb", [P, H])
        w_out_sb = sb("w_out_sb", [P, H, D])
        eps_sb = sb("eps_sb", [P, 2])
        bias_sb = sb("bias_sb", [P, 2, LAYERS])
        stats = sb("stats", [P, RG, 6])
        stat_in = sb("stat_in", [P, 1])
        mv = sb("mv", [P, RG, 2])
        ve = sb("ve", [P, RG])
        rs = sb("rs", [P, RG])
        stats2 = sb("stats2", [P, RG, 6])
        mv2 = sb("mv2", [P, RG, 2])
        ve2 = sb("ve2", [P, RG])
        rs2 = sb("rs2", [P, RG])
        res = [sb(f"res{i}", [P, RG, D]) for i in range(2)]

        A = ExitStack()
        xh = [sb(f"xh{k}", [P, KB, D], F32R, A) for k in range(2)]
        xl = [sb(f"xl{k}", [P, KB, D], F32R, A) for k in range(2)]
        ah = [sb(f"ah{k}", [P, CHC], F32R, A) for k in range(2)]
        al = [sb(f"al{k}", [P, CHC], F32R, A) for k in range(2)]
        rows = [sb(f"rows{k}", [P, GROUPS, PC], F32, A) for k in range(2)]
        at = [sb(f"at{k}", [P, CH, TILE], F32, A) for k in range(2)]
        w_nat = sb("w_nat", [P, 2 * LAYERS + 2, D], F32, A)
        w_T = sb("w_T", [P, 2 * LAYERS + 2, D], F32, A)
        A1 = ExitStack()
        xs = [sb(f"xs{k}", [P, KB, D], F32, A1) for k in range(2)]
        A1.close()
        hid = [[sb(f"hid{k}_{l}", [P, TILE], F32, A) for l in range(LAYERS + 1)] for k in range(2)]
        ysum = sb("ysum", [P, RG, D], F32, A)
        xn = sb("xn", [P, RG, D], F32, A)
        A.close()

        B = ExitStack()
        xm = sb("xm", [P, KB, D], F32, B)
        NADJ = 4
        adjc = [sb(f"adjc{k}", [P, CH, TILE], F32, B) for k in range(NADJ)]
        axT = sb("axT", [P, TILE], F32, B)
        g = sb("g", [P, RG, D], F32, B)
        hn = sb("hn", [P, RG, D], F32, B)
        hT = sb("hT", [P, TILE], F32, B)
        xc = sb("xc", [P, H, TILE + TAPS], F32, B)
        cv = sb("cv", [P, H, TILE], F32, B)
        u = [sb(f"u{k}", [P, H, TILE], F32, B) for k in range(2)]
        sz = [sb(f"sz{k}", [P, H, TILE], F32, B) for k in range(2)]
        sp_a = sb("sp_a", [P, H, TILE], F32, B)
        sp_r = sb("sp_r", [P, H, TILE], F32, B)
        dt_ = [sb(f"dt{k}", [P, H, TILE], F32, B) for k in range(2)]
        dtu = [sb(f"dtu{k}", [P, H, TILE], F32, B) for k in range(2)]
        dtr = sb("dtr", [P, TILE], F32, B)
        bc = [sb(f"bc{k}", [P, TILE], F32R, B) for k in range(2)]
        sel = sb("sel", [P, 2 * S, P], F32R, B)
        NDA, NPR = 4, 4
        dA = [sb(f"dA{k}", [P, H, TILE], F32, B) for k in range(NDA)]
        dBuV = [sb(f"dBuV{k}", [P, H, TILE], F32, B) for k in range(2)]
        dBuP = sb("dBuP", [P, H, TILE], F32, B)
        hs = [sb(f"hs{k}", [P, H, TILE], F32, B) for k in range(2)]
        pr = [sb(f"pr{k}", [P, H, TILE], F32, B) for k in range(NPR)]
        y = [sb(f"y{k}", [P, H, TILE], F32, B) for k in range(2)]
        b_sb = [sb(f"b_sb{k}", [P, TILE], F32, B) for k in range(2)]
        state = sb("state", [P, S, H], F32, B)
        o_s = sb("o_s", [P, RG, D], F32, B)
        o_n = sb("o_n", [P, RG, D], F32, B)
        B.close()

        bank = [ctx.enter_context(nc.psum_tensor(f"bank{i}", [P, TILE], F32)) for i in range(8)]
        acc = [bank[0], bank[1]]
        lay = [bank[2], bank[3]]
        mrg = bank[4][:, :].rearrange("p (g d) -> p g d", g=RG)
        accB, M0, M1 = bank[0], bank[1], bank[2]
        BB = [bank[3], bank[5]]
        CC = [bank[4], bank[6]]
        O = bank[7][:, :].rearrange("p (g d) -> p g d", g=RG)
        M0g = M0[:, :].rearrange("p (g d) -> p g d", g=RG)

        s_w = sem("s_w")
        s_ident = sem("s_ident")
        s_xload = [sem(f"s_xload{k}") for k in range(2)]
        s_xhi, s_xlo = sem("s_xhi"), sem("s_xlo")
        s_wTp, s_wT = sem("s_wTp"), sem("s_wT")
        s_rows = [sem(f"s_rows{k}") for k in range(2)]
        s_rowsfree = sem("s_rowsfree")
        s_at = sem("s_at")
        s_atout = [sem(f"s_atout{k}") for k in range(2)]
        s_ah, s_al = sem("s_ah"), sem("s_al")
        s_used = sem("s_used")
        s_acc = [sem(f"s_acc{k}") for k in range(2)]
        s_h0 = [sem(f"s_h0{k}") for k in range(2)]
        s_lay, s_hid = sem("s_lay"), sem("s_hid")
        s_mrg, s_ya, s_yb, s_st, s_mv = sem("s_mrg"), sem("s_ya"), sem("s_yb"), sem("s_st"), sem("s_mv")
        s_ve, s_rs, s_xn, s_mid = sem("s_ve"), sem("s_rs"), sem("s_xn"), sem("s_mid")
        s_res = sem("s_res")
        b_res = [sem(f"b_res{k}") for k in range(2)]
        s_prepA = sem("s_prepA")
        s_aend = sem("s_aend")

        b_xm = sem("b_xm")
        b_adj = [sem(f"b_adj{k}") for k in range(NADJ)]
        b_adjused, b_acc, b_ax = sem("b_adjused"), sem("b_acc"), sem("b_ax")
        b_gcn, b_g, b_relu, b_st, b_mv, b_ve, b_rs, b_hn = [sem(f"b_{n}") for n in "gcn g relu st mv ve rs hn".split()]
        b_tr, b_hT, b_xc, b_hist, b_xcev, b_conv, b_cvstep = [sem(f"b_{n}") for n in "tr hT xc hist xcev conv cvstep".split()]
        b_z, b_u, b_sz, b_dbc, b_bchi, b_bc, b_dtp = [sem(f"b_{n}") for n in "z u sz dbc bchi bc dtp".split()]
        b_spab, b_spe, b_spw, b_spl, b_spd, b_sps, b_dtv, b_dtu = [sem(f"b_{n}") for n in "spab spe spw spl spd sps dtv dtu".split()]
        b_B, b_C, b_Bsb, b_dA = [sem(f"b_{n}") for n in "B C Bsb dA".split()]
        b_dbuV, b_dbuP, b_scan, b_state, b_p, b_y = [sem(f"b_{n}") for n in "dbuV dbuP scan state p y".split()]
        b_yd, b_yg, b_out, b_os, b_ost, b_omv, b_ove, b_ors, b_on = [sem(f"b_{n}") for n in "yd yg out os ost omv ove ors on".split()]
        b_store = sem("b_store")
        b_zero = sem("b_zero")
        b_sel = sem("b_sel")

        WLOADS = 30

        def nB(n):
            return sum(1 for k in POOL_B if k < n)

        NPB = len(POOL_B)
        NVB = S - NPB

        block = ctx.enter_context(nc.Block())

        def load_rows(eng, quads, it, r):
            for q in quads:
                col = q * (N // Q) + r * PC
                src = adj[bass.ds(it * TILE, TILE), col:col + PC].rearrange("(g i) c -> i g c", g=GROUPS)
                eng.dma_start(rows[r % 2][32 * q:32 * q + 32, :, :], src).then_inc(s_rows[r % 2], 16)

        @block.sync
        def _(sp):
            for k, src in enumerate((x, x2)):
                v = src.rearrange("(q m i) d -> q i m d", q=Q, i=32)
                for q in range(Q):
                    sp.dma_start(xs[k][32 * q:32 * q + 32, :, :], v[q]).then_inc(s_xload[k], 16)
                if k == 0:
                    load_rows(sp, (0, 1), 0, 0)
            load_rows(sp, (0, 1), 0, 1)

            def stage_a(it, last):
                for r in range(PIECES):
                    for c in (2 * r, 2 * r + 1):
                        sp.wait_ge(s_at, CHUNKS * it + c + 1)
                        sp.dma_start(adjT[bass.ds((it * CHUNKS + c) * P, P), :],
                                     at[c % 2][:, :, :].rearrange("p m t -> p (m t)")).then_inc(s_atout[c % 2], 16)
                    if not (last and r >= 2):
                        sp.wait_ge(s_rowsfree, PIECES * it + r + 1)
                        load_rows(sp, (0, 1), it + (r + 2) // PIECES, (r + 2) % PIECES)

            with sp.Fori(0, TILES - 1) as it:
                stage_a(it, False)
            stage_a(TILES - 1, True)

            for k in range(2):
                sp.wait_ge(s_atout[k], 16 * TILES * CHUNKS // 2)
            sp.sem_inc(s_aend, 1)
            sp.wait_ge(s_aend, 5)
            vm = mid.rearrange("(q m i) d -> q i m d", q=Q, i=32)
            for q in range(Q):
                sp.dma_start(xm[32 * q:32 * q + 32, :, :], vm[q]).then_inc(b_xm, 16)

            def load_adj(a, chunks):
                for c in chunks:
                    wait(sp, b_adjused, CHUNKS * a + c - NADJ + 1)
                    sp.dma_start(adjc[c % NADJ][:, :, :].rearrange("p m t -> p (m t)"),
                                 adjT[bass.ds((a * CHUNKS + c) * P, P), :]).then_inc(b_adj[c % NADJ], 16)

            def load_res(b, par):
                wait(sp, b_os, b - 1)
                sp.dma_start(res[par][:, :, :], mid[bass.ds(b * TILE, TILE), :].rearrange("(g p) d -> p g d", g=RG))\
                    .then_inc(b_res[par], 16)

            def store(b):
                sp.wait_ge(b_on, b + 1)
                sp.dma_start(out[bass.ds(b * TILE, TILE), :].rearrange("(g p) d -> p g d", g=RG), o_n[:, :, :])\
                    .then_inc(b_store, 16)

            def window(b, par, tail, adj_):
                load_res(b, par)
                if adj_:
                    load_adj(b + 2, range(0, CHUNKS - 2))
                if tail:
                    store(b - 1)
                if adj_:
                    load_adj(b + 2, range(CHUNKS - 2, CHUNKS))

            load_adj(0, range(CHUNKS))
            load_adj(1, range(CHUNKS))
            window(0, 0, False, True)
            with sp.Fori(0, 2) as i:
                window(2 * i + 1, 1, True, True)
                window(2 * i + 2, 0, True, True)
            window(5, 1, True, True)
            window(6, 0, True, False)
            window(7, 1, True, False)
            store(TILES - 1)
            sp.wait_ge(b_store, 16 * TILES)

        @block.gpsimd
        def _(pool):
            loads = []

            def load(dst, src):
                loads.append(dst)
                pool.dma_start(dst, src).then_inc(s_w, 16)

            load(w_nat[:, 0:LAYERS, :], W1.rearrange("l o d -> o l d"))
            load(w_nat[:, LAYERS:2 * LAYERS, :], W2.rearrange("l o d -> o l d"))
            load(w_nat[:, 2 * LAYERS:, :].rearrange("p k d -> p (k d)"), Wm)
            for k, b in enumerate((b1, b2)):
                for l in range(LAYERS):
                    load(bias_sb[:, k, l:l + 1], b[l].rearrange("(p o) -> p o", o=1))
            load(eps_sb[:, 0:1], eps1.partition_broadcast(P))
            load(eps_sb[:, 1:2], eps2.partition_broadcast(P))
            load(bm_sb[:, :], bm.partition_broadcast(P))
            load(gcn_b_sb[:, :], gcn_b.partition_broadcast(P))
            load(gcn_w_sb[:, :], gcn_w)
            load(ln_g_sb[:, :], ln_g.rearrange("(p o) -> p o", o=1))
            load(ln_b_sb[:, :], ln_b.rearrange("(p o) -> p o", o=1))
            load(w_in_sb[:, :], w_in)
            load(conv_w_sb[:, :, :], conv_w.rearrange("(h p) k -> p h k", h=H))
            load(w_dt_sb[64:64 + R, :], w_dt)
            load(A_sb[:, :, :], A_log.rearrange("(h p) s -> p h s", h=H))
            load(w_out_sb[:, :, :], w_out.rearrange("(h p) d -> p h d", h=H))
            for h in range(H):
                for dst, src in ((conv_b_sb, conv_b), (b_dt_sb, b_dt), (D_sb, D_skip)):
                    load(dst[:, h:h + 1], src.rearrange("(h p o) -> h p o", h=H, o=1)[h])
            v = w_xp.rearrange("(h p) j -> p h j", h=H)
            load(w_xp_sb[:, :, 0:2 * S], v[:, :, R:])
            load(w_xp_sb[:, :, 2 * S:4 * S], v[:, :, R:])
            load(w_xp_sb[:, :, 4 * S:], v[:, :, 0:R])

            assert len(loads) == WLOADS

            nc.gpsimd.memset(ident[:, :], 0.0).then_inc(s_ident, 1)
            pool.wait_ge(s_ident, 1)
            nc.gpsimd.affine_select(out=ident[:, :], in_=ident[:, :], compare_op=ALU.not_equal, fill=1.0, base=0,
                                    pattern=[[-1, P]], channel_multiplier=1).then_inc(s_ident, 1)
            nc.gpsimd.memset(neg_half[:, :], -0.5).then_inc(s_ident, 1)
            nc.gpsimd.memset(eps_ln[:, :], EPS).then_inc(s_ident, 1)
            pool.wait_ge(s_ident, 4)

            def load_res(it, par):
                pool.dma_start(res[par][:, :, :], x[bass.ds(it * TILE, TILE), :].rearrange("(g p) d -> p g d", g=RG))\
                    .then_inc(s_res, 16)

            def norm(it):
                pool.wait_ge(s_mv, it + 1)
                nc.gpsimd.tensor_tensor(ve[:, :], mv[:, :, 1], eps_ln[:, :], ALU.add).then_inc(s_ve, 1)
                pool.wait_ge(s_ve, it + 1)
                nc.gpsimd.tensor_tensor(rs[:, :], ve[:, :], neg_half[:, :], ALU.pow).then_inc(s_rs, 1)
                pool.wait_ge(s_xn, it + 1)
                pool.dma_start(mid[bass.ds(it * TILE, TILE), :].rearrange("(g p) d -> p g d", g=RG), xn[:, :, :])\
                    .then_inc(s_mid, 16)

            load_res(0, 0)
            with pool.Fori(0, TILES - 1) as it:
                norm(it)
                load_res(it + 1, 0)
            norm(TILES - 1)

            pool.wait_ge(s_mid, 16 * TILES)
            pool.sem_inc(s_aend, 1)
            pool.wait_ge(s_aend, 5)
            nc.gpsimd.memset(state[:, :, :], 0.0).then_inc(b_zero, 1)
            nc.gpsimd.memset(xc[:, :, :], 0.0).then_inc(b_zero, 1)

            def front_rs(a):
                pool.wait_ge(b_mv, a + 1)
                nc.gpsimd.tensor_tensor(ve[:, :], mv[:, :, 1], eps_ln[:, :], ALU.add).then_inc(b_ve, 1)
                pool.wait_ge(b_ve, a + 1)
                nc.gpsimd.tensor_tensor(rs[:, :], ve[:, :], neg_half[:, :], ALU.pow).then_inc(b_rs, 1)

            def front_dt(a, par, step):
                if step == 0:
                    pool.wait_ge(b_spd, a + 1)
                    nc.gpsimd.tensor_tensor(dt_[par][:, :, :], dt_[par][:, :, :], sp_a[:, :, :], ALU.subtract)\
                        .then_inc(b_sps, 1)
                elif step == 1:
                    pool.wait_ge(b_sps, a + 1)
                    nc.gpsimd.tensor_tensor(dt_[par][:, :, :], dt_[par][:, :, :], sp_r[:, :, :], ALU.add).then_inc(b_dtv, 1)
                else:
                    pool.wait_ge(b_dtv, a + 1)
                    nc.gpsimd.tensor_tensor(dtu[par][:, :, :], dt_[par][:, :, :], u[par][:, :, :], ALU.mult)\
                        .then_inc(b_dtu, 1)

            def tail_gate(b, par):
                pool.wait_ge(b_yd, b + 1)
                nc.gpsimd.tensor_tensor(y[par][:, :, :], y[par][:, :, :], sz[par][:, :, :], ALU.mult).then_inc(b_yg, 1)

            def tail_rs(b):
                pool.wait_ge(b_omv, b + 1)
                nc.gpsimd.tensor_tensor(ve2[:, :], mv2[:, :, 1], eps_ln[:, :], ALU.add).then_inc(b_ove, 1)
                pool.wait_ge(b_ove, b + 1)
                nc.gpsimd.tensor_tensor(rs2[:, :], ve2[:, :], neg_half[:, :], ALU.pow).then_inc(b_ors, 1)

            def window(b, par, tail, front):
                for n in range(S + 2):
                    if n in POOL_B:
                        pool.wait_ge(b_Bsb, NPB * b + nB(n) + 1)
                        before = max([k for k in POOL_B if k < n], default=POOL_B[-1] - S)
                        wait(pool, b_scan, H * (S * b + before + 1))
                        pool.wait_ge(b_dtu, b + 1)
                        nc.gpsimd.tensor_tensor(dBuP[:, :, :], dtu[par][:, :, :],
                                                b_sb[b_slot(n, par)][:, :].unsqueeze(1).to_broadcast([P, H, TILE]),
                                                ALU.mult).then_inc(b_dbuP, 1)
                    k = n - 2
                    if k == 1:
                        wait(pool, b_out, b - 1)
                        pool.wait_ge(b_p, S * b + 2)
                        nc.gpsimd.tensor_tensor(y[par][:, :, :], pr[0][:, :, :], pr[1][:, :, :], ALU.add).then_inc(b_y, 1)
                    elif k > 1:
                        pool.wait_ge(b_p, S * b + k + 1)
                        pool.wait_ge(b_y, (S - 1) * b + k - 1)
                        nc.gpsimd.tensor_tensor(y[par][:, :, :], y[par][:, :, :], pr[k % NPR][:, :, :], ALU.add).then_inc(b_y, 1)
                    if front and n == 1:
                        front_rs(b + 1)
                    if tail and n == 3:
                        tail_gate(b - 1, 1 - par)
                    if tail and n == 6:
                        tail_rs(b - 1)
                    if front and n in (12, 13, 14):
                        front_dt(b + 1, 1 - par, n - 12)

            def b_slot(n, par):
                return (nB(n) + NPB * par) % 2

            front_rs(0)
            for step in range(3):
                front_dt(0, 0, step)
            window(0, 0, False, True)
            with pool.Fori(0, 2) as i:
                window(2 * i + 1, 1, True, True)
                window(2 * i + 2, 0, True, True)
            window(5, 1, True, True)
            window(6, 0, True, True)
            window(7, 1, True, False)
            tail_gate(TILES - 1, 1)
            tail_rs(TILES - 1)

        @block.scalar
        def _(act):
            load_rows(act, (2, 3), 0, 0)
            load_rows(act, (2, 3), 0, 1)
            for k in range(2):
                act.wait_ge(s_xload[k], 16 * Q)
                nc.scalar.activation(xh[k][:, :, :], xs[k][:, :, :], ACT.Copy).then_inc(s_xhi, 1)
            act.wait_ge(s_w, 16 * WLOADS)
            nc.scalar.activation(eps_sb[:, :], eps_sb[:, :], ACT.Identity, bias=2.0).then_inc(s_prepA, 1)

            def hi(it, c):
                n = CHUNKS * it + c
                act.wait_ge(s_at, n + 1)
                wait(act, s_used, n - 1)
                nc.scalar.activation(ah[c % 2][:, :], at[c % 2][:, :, :].rearrange("p m t -> p (m t)"), ACT.Copy)\
                    .then_inc(s_ah, 1)

            def first(it):
                for k in range(2):
                    act.wait_ge(s_acc[k], it + 1)
                    nc.scalar.activation(hid[k][0][:, :], acc[k][:, :], ACT.Identity, scale=eps_sb[:, k:k + 1])\
                        .then_inc(s_h0[k], 1)

            def layer(it, l):
                for k in range(2):
                    act.wait_ge(s_lay, 2 * (LAYERS * it + l) + k + 1)
                    nc.scalar.activation(hid[k][l + 1][:, :], lay[k][:, :], ACT.Relu, bias=bias_sb[:, k, l:l + 1])\
                        .then_inc(s_hid, 1)

            def stage_a(it, mlp, last):
                for c in range(CHUNKS):
                    hi(it, c)
                    if c % 2 and not (last and c >= 4):
                        r = c // 2
                        act.wait_ge(s_rowsfree, PIECES * it + r + 1)
                        load_rows(act, (2, 3), it + (r + 2) // PIECES, (r + 2) % PIECES)
                    if mlp and c == 0:
                        first(it - 1)
                    if mlp and c in (2, 3, 4):
                        layer(it - 1, c - 2)

            act.wait_ge(s_prepA, 1)
            stage_a(0, False, False)
            with act.Fori(1, TILES - 1) as it:
                stage_a(it, True, False)
            stage_a(TILES - 1, True, True)
            first(TILES - 1)
            for l in range(LAYERS):
                layer(TILES - 1, l)

            act.wait_ge(s_xn, TILES)
            act.sem_inc(s_aend, 1)
            act.wait_ge(s_aend, 5)
            act.preload_act_table_set("natural_log_exp_and_others")
            nc.scalar.activation(A_sb[:, :, :], A_sb[:, :, :], ACT.Exp).then_inc(s_prepA, 1)
            act.wait_ge(s_prepA, 2)
            nc.scalar.activation(A_sb[:, :, :], A_sb[:, :, :], ACT.Copy, scale=-1.0).then_inc(s_prepA, 1)
            act.wait_ge(s_prepA, 3)
            act.wait_ge(b_zero, 2)
            act.wait_ge(s_ident, 4)
            for half in range(2):
                blk = slice(32 * half, 32 * half + 32)
                nc.scalar.activation(sel[blk, :, :], ident[blk, blk].unsqueeze(2).to_broadcast([32, 2 * S, P]),
                                     ACT.Copy).then_inc(b_sel, 1)

            def front_ax(a):
                act.wait_ge(b_acc, a + 1)
                wait(act, b_gcn, a)
                nc.scalar.activation(axT[:, :], accB[:, :], ACT.Copy).then_inc(b_ax, 1)

            def front_hT(a):
                act.wait_ge(b_tr, a + 1)
                wait(act, b_z, a)
                nc.scalar.activation(hT[:, :], M1[:, :], ACT.Identity, bias=ln_b_sb[:, :], scale=ln_g_sb[:, :])\
                    .then_inc(b_hT, 1)

            def front_xc(a):
                act.wait_ge(b_xc, a + 1)
                wait(act, b_conv, a)
                wait(act, b_u, a)
                nc.scalar.activation(xc[:, :, 0:TAPS - 1], xc[:, :, TILE:TILE + TAPS - 1], ACT.Copy).then_inc(b_hist, 1)
                act.wait_ge(b_hist, a + 1)
                for h, m in enumerate((M0, M1)):
                    nc.scalar.activation(xc[:, h, TAPS - 1:TILE + TAPS - 1], m[:, :], ACT.Copy).then_inc(b_xcev, 1)
                    nc.scalar.activation(cv[:, h, :], m[:, :], ACT.Identity, bias=conv_b_sb[:, h:h + 1],
                                         scale=conv_w_sb[:, h, TAPS - 1:TAPS]).then_inc(b_xcev, 1)

            def front_silu(a, par):
                act.wait_ge(b_conv, a + 1)
                wait(act, b_yd, a - 1)
                wait(act, b_yg, a - 1)
                nc.scalar.activation(u[par][:, :, :], cv[:, :, :], ACT.Silu).then_inc(b_u, 1)
                act.wait_ge(b_z, a + 1)
                for h, m in enumerate((M0, M1)):
                    nc.scalar.activation(sz[par][:, h, :], m[:, :], ACT.Silu).then_inc(b_sz, 1)
                act.preload_act_table_set("natural_log_exp_and_others")

            def front_bc(a, par):
                act.wait_ge(b_dbc, a + 1)
                wait(act, b_C, S * (a - 1))
                wait(act, b_dtp, 2 * a)
                nc.scalar.activation(bc[par][0:4 * S, :], M0[0:4 * S, :], ACT.Copy).then_inc(b_bchi, 1)
                nc.scalar.activation(dtr[4 * S:4 * S + R, :], M0[4 * S:4 * S + R, :], ACT.Copy).then_inc(b_bchi, 1)

            def front_sp(a, par):
                act.wait_ge(b_dtp, 2 * a + 2)
                wait(act, b_dtv, a)
                for h, m in enumerate((M1, M0)):
                    nc.scalar.activation(sp_a[:, h, :], m[:, :], ACT.Abs, bias=b_dt_sb[:, h:h + 1]).then_inc(b_spab, 1)
                    nc.scalar.activation(sp_r[:, h, :], m[:, :], ACT.Relu, bias=b_dt_sb[:, h:h + 1]).then_inc(b_spab, 1)
                act.wait_ge(b_spab, 4 * a + 4)
                nc.scalar.activation(sp_a[:, :, :], sp_a[:, :, :], ACT.Exp, scale=-1.0).then_inc(b_spe, 1)
                act.wait_ge(b_spe, a + 1)
                nc.scalar.activation(dtu[par][:, :, :], sp_a[:, :, :], ACT.Identity, bias=1.0).then_inc(b_spw, 1)
                act.wait_ge(b_spw, a + 1)
                nc.scalar.activation(dt_[par][:, :, :], dtu[par][:, :, :], ACT.Ln).then_inc(b_spl, 1)

            def window(b, par, front):
                for n in range(S + NDA):
                    k = n - NDA
                    if k >= 0:
                        act.wait_ge(b_scan, H * (S * b + k + 1))
                        nc.scalar.activation(state[:, k, :], hs[k % 2][:, :, TILE - 1], ACT.Copy).then_inc(b_state, 1)
                    if n < S:
                        if n == 0:
                            act.wait_ge(b_dtv, b + 1)
                        wait(act, b_scan, H * (S * b + n - NDA + 1))
                        for h in range(H):
                            nc.scalar.activation(dA[n % NDA][:, h, :], dt_[par][:, h, :], ACT.Exp,
                                                 scale=A_sb[:, h, n:n + 1]).then_inc(b_dA, 1)
                    k = n - 2
                    if k in POOL_B:
                        act.wait_ge(b_B, S * b + k + 1)
                        wait(act, b_dbuP, NPB * b + nB(k) - 1)
                        nc.scalar.activation(b_sb[(nB(k) + NPB * par) % 2][:, :], BB[k % 2][:, :], ACT.Copy).then_inc(b_Bsb, 1)
                    if front:
                        if n == 0:
                            front_ax(b + 1)
                        if n == 6:
                            front_hT(b + 1)
                        if n == 8:
                            front_xc(b + 1)
                        if n == 10:
                            front_silu(b + 1, 1 - par)
                        if n == 12:
                            front_bc(b + 1, 1 - par)
                        if n == 14:
                            front_sp(b + 1, 1 - par)

            front_ax(0)
            front_hT(0)
            front_xc(0)
            front_silu(0, 0)
            front_bc(0, 0)
            front_sp(0, 0)
            window(0, 0, True)
            with act.Fori(0, 2) as i:
                window(2 * i + 1, 1, True)
                window(2 * i + 2, 0, True)
            window(5, 1, True)
            window(6, 0, True)
            window(7, 1, False)

        @block.vector
        def _(dve):
            for k in range(2):
                dve.wait_ge(s_xhi, k + 1)
                nc.vector.tensor_tensor(xl[k][:, :, :], xs[k][:, :, :], xh[k][:, :, :], ALU.subtract).then_inc(s_xlo, 1)
            for k in range(2):
                dve.wait_ge(s_wTp, 4 * (k + 1))
                nc.vector.tensor_copy(w_T[:, 4 * k:4 * k + 4, :].rearrange("p a b -> p (a b)"), bank[5 + k][:, :])\
                    .then_inc(s_wT, 1)

            def transpose(it, c):
                n = CHUNKS * it + c
                piece = rows[(c // 2) % 2]
                if c % 2 == 0:
                    dve.wait_ge(s_rows[(c // 2) % 2], 64 * (2 * it + c // 4 + 1))
                wait(dve, s_al, n - 1)
                wait(dve, s_atout[c % 2], 16 * (CHUNKS // 2 * it + c // 2))
                half = GROUPS // 2
                for j in range(2):
                    src = piece[:, half * j:half * j + half, P * (c % 2):P * (c % 2) + P]
                    dst = at[c % 2][:, :, 32 * half * j:32 * half * (j + 1)]
                    last = nc.vector.transpose(dst.rearrange("p m (g i) -> p g m i", i=32),
                                               src.rearrange("p g (m i) -> p g m i", i=32))
                last.then_inc(s_at, 1)
                if c % 2:
                    dve.wait_ge(s_at, n + 1)
                    dve.sem_inc(s_rowsfree, 1)

            def lo(it, c):
                n = CHUNKS * it + c
                dve.wait_ge(s_ah, n + 1)
                wait(dve, s_used, n - 1)
                nc.vector.tensor_tensor(al[c % 2][:, :], at[c % 2][:, :, :].rearrange("p m t -> p (m t)"),
                                        ah[c % 2][:, :], ALU.subtract).then_inc(s_al, 1)

            def norm_stats(it):
                dve.wait_ge(s_mrg, it + 1)
                nc.vector.tensor_tensor(ysum[:, :, :], mrg, bm_sb[:, :].unsqueeze(1).to_broadcast([P, RG, D]), ALU.add)\
                    .then_inc(s_ya, 1)
                dve.wait_ge(s_ya, it + 1)
                dve.wait_ge(s_res, 16 * it + 16)
                nc.vector.tensor_tensor(ysum[:, :, :], ysum[:, :, :], res[0][:, :, :], ALU.add).then_inc(s_yb, 1)
                dve.wait_ge(s_yb, it + 1)
                for q in range(RG):
                    last = nc.vector.bn_stats(stats[:, q, :], ysum[:, q, :])
                last.then_inc(s_st, 1)
                dve.wait_ge(s_st, it + 1)
                nc.vector.tensor_copy(stat_in[:, :], stats[:, 0, 0:1])
                for q in range(RG):
                    last = nc.vector.bn_aggr(mv[:, q, :], stats[:, q, :])
                last.then_inc(s_mv, 1)

            def norm_apply(it):
                dve.wait_ge(s_rs, it + 1)
                wait(dve, s_mid, 16 * it)
                for q in range(RG):
                    last = nc.vector.tensor_scalar(xn[:, q, :], ysum[:, q, :], mv[:, q, 0:1], rs[:, q:q + 1],
                                                   ALU.subtract, ALU.mult)
                last.then_inc(s_xn, 1)

            def stage_a(it, mlp):
                for c in range(CHUNKS):
                    transpose(it, c)
                    if c > 0:
                        lo(it, c - 1)
                    elif mlp:
                        lo(it - 1, CHUNKS - 1)
                    if mlp and c == 6:
                        norm_stats(it - 1)
                    if mlp and c == 7:
                        norm_apply(it - 1)

            stage_a(0, False)
            with dve.Fori(1, TILES) as it:
                stage_a(it, True)
            lo(TILES - 1, CHUNKS - 1)
            norm_stats(TILES - 1)
            norm_apply(TILES - 1)

            dve.wait_ge(s_xn, TILES)
            dve.sem_inc(s_aend, 1)
            dve.wait_ge(s_aend, 5)
            dve.wait_ge(b_zero, 2)

            def front_g(a):
                dve.wait_ge(b_gcn, a + 1)
                wait(dve, b_hn, a)
                nc.vector.tensor_tensor(g[:, :, :], M0g, gcn_b_sb[:, :].unsqueeze(1).to_broadcast([P, RG, D]), ALU.add)\
                    .then_inc(b_g, 1)
                dve.wait_ge(b_g, a + 1)
                nc.vector.tensor_scalar(g[:, :, :], g[:, :, :], 0.0, None, ALU.max).then_inc(b_relu, 1)
                dve.wait_ge(b_relu, a + 1)
                for q in range(RG):
                    last = nc.vector.bn_stats(stats[:, q, :], g[:, q, :])
                last.then_inc(b_st, 1)
                dve.wait_ge(b_st, a + 1)
                nc.vector.tensor_copy(stat_in[:, :], stats[:, 0, 0:1])
                for q in range(RG):
                    last = nc.vector.bn_aggr(mv[:, q, :], stats[:, q, :])
                last.then_inc(b_mv, 1)

            def front_hn(a):
                dve.wait_ge(b_rs, a + 1)
                wait(dve, b_tr, a)
                for q in range(RG):
                    last = nc.vector.tensor_scalar(hn[:, q, :], g[:, q, :], mv[:, q, 0:1], rs[:, q:q + 1],
                                                   ALU.subtract, ALU.mult)
                last.then_inc(b_hn, 1)

            def front_conv(a):
                dve.wait_ge(b_xcev, 4 * a + 4)
                for k in range(TAPS - 1):
                    for h in range(H):
                        if k > 0:
                            dve.wait_ge(b_cvstep, 4 * a + 2 * (k - 1) + h + 1)
                        last = nc.vector.scalar_tensor_tensor(cv[:, h, :], xc[:, h, k:k + TILE], conv_w_sb[:, h, k:k + 1],
                                                              cv[:, h, :], ALU.mult, ALU.add)
                        if k < TAPS - 2:
                            last.then_inc(b_cvstep, 1)
                last.then_inc(b_conv, 1)

            def front_bclo(a, par):
                dve.wait_ge(b_bchi, 2 * a + 2)
                nc.vector.tensor_tensor(bc[par][2 * S:4 * S, :], M0[2 * S:4 * S, :], bc[par][2 * S:4 * S, :], ALU.subtract)\
                    .then_inc(b_bc, 1)

            def front_spd(a, par):
                dve.wait_ge(b_spl, a + 1)
                nc.vector.scalar_tensor_tensor(sp_a[:, :, :], dtu[par][:, :, :], -1.0, sp_a[:, :, :], ALU.add, ALU.subtract)\
                    .then_inc(b_spd, 1)

            def tail_y(b, par):
                dve.wait_ge(b_y, (S - 1) * (b + 1))
                for h in range(H):
                    last = nc.vector.scalar_tensor_tensor(y[par][:, h, :], u[par][:, h, :], D_sb[:, h:h + 1], y[par][:, h, :],
                                                          ALU.mult, ALU.add)
                last.then_inc(b_yd, 1)

            def tail_stats(b, par):
                dve.wait_ge(b_out, b + 1)
                dve.wait_ge(b_res[par], 8 * (b - par) + 16)
                nc.vector.tensor_tensor(o_s[:, :, :], O, res[par][:, :, :], ALU.add).then_inc(b_os, 1)
                dve.wait_ge(b_os, b + 1)
                for q in range(RG):
                    last = nc.vector.bn_stats(stats2[:, q, :], o_s[:, q, :])
                last.then_inc(b_ost, 1)
                dve.wait_ge(b_ost, b + 1)
                nc.vector.tensor_copy(stat_in[:, :], stats2[:, 0, 0:1])
                for q in range(RG):
                    last = nc.vector.bn_aggr(mv2[:, q, :], stats2[:, q, :])
                last.then_inc(b_omv, 1)

            def tail_norm(b):
                dve.wait_ge(b_ors, b + 1)
                wait(dve, b_store, 16 * b)
                for q in range(RG):
                    last = nc.vector.tensor_scalar(o_n[:, q, :], o_s[:, q, :], mv2[:, q, 0:1], rs2[:, q:q + 1],
                                                   ALU.subtract, ALU.mult)
                last.then_inc(b_on, 1)

            def v_slot(n, par):
                return (n - nB(n) + NVB * par) % 2

            def window(b, par, tail, front):
                for n in range(S + 2):
                    if n < S and n not in POOL_B:
                        dve.wait_ge(b_B, S * b + n + 1)
                        if n == 0:
                            dve.wait_ge(b_dtu, b + 1)
                        wait(dve, b_scan, H * (S * b + n - 1))
                        nc.vector.tensor_tensor(dBuV[v_slot(n, par)][:, :, :], dtu[par][:, :, :],
                                                BB[n % 2][:, :].unsqueeze(1).to_broadcast([P, H, TILE]), ALU.mult)\
                            .then_inc(b_dbuV, 1)
                    k = n - 1
                    if 0 <= k < S:
                        dve.wait_ge(b_dA, H * (S * b + k + 1))
                        if k in POOL_B:
                            dve.wait_ge(b_dbuP, NPB * b + nB(k) + 1)
                        else:
                            dve.wait_ge(b_dbuV, NVB * b + k - nB(k) + 1)
                        wait(dve, b_state, S * b + k - 1)
                        wait(dve, b_p, S * b + k - 1)
                        src = dBuP if k in POOL_B else dBuV[v_slot(k, par)]
                        for h in range(H):
                            nc.vector.tensor_tensor_scan(hs[k % 2][:, h, :], dA[k % NDA][:, h, :], src[:, h, :],
                                                         state[:, k, h:h + 1], ALU.mult, ALU.add).then_inc(b_scan, 1)
                    k = n - 2
                    if k >= 0:
                        dve.wait_ge(b_C, S * b + k + 1)
                        dve.wait_ge(b_scan, H * (S * b + k + 1))
                        wait(dve, b_y, (S - 1) * b + (max(k - NPR, 1) if k >= NPR else k - NPR + 1))
                        nc.vector.tensor_tensor(pr[k % NPR][:, :, :], hs[k % 2][:, :, :],
                                                CC[k % 2][:, :].unsqueeze(1).to_broadcast([P, H, TILE]), ALU.mult)\
                            .then_inc(b_p, 1)
                    if front:
                        if n == 1:
                            front_g(b + 1)
                        if n == 2:
                            front_hn(b + 1)
                        if n == 6:
                            front_conv(b + 1)
                        if n == 9:
                            front_bclo(b + 1, 1 - par)
                        if n == 12:
                            front_spd(b + 1, 1 - par)
                    if tail:
                        if n == 3:
                            tail_y(b - 1, 1 - par)
                        if n == 5:
                            tail_stats(b - 1, 1 - par)
                        if n == 7:
                            tail_norm(b - 1)

            front_g(0)
            front_hn(0)
            front_conv(0)
            front_bclo(0, 0)
            front_spd(0, 0)
            window(0, 0, False, True)
            with dve.Fori(0, 2) as i:
                window(2 * i + 1, 1, True, True)
                window(2 * i + 2, 0, True, True)
            window(5, 1, True, True)
            window(6, 0, True, True)
            window(7, 1, True, False)
            tail_y(TILES - 1, 1)
            tail_stats(TILES - 1, 1)
            tail_norm(TILES - 1)

        @block.tensor
        def _(pe):
            mm = nc.tensor.matmul
            pe.wait_ge(s_w, 16 * WLOADS)
            pe.wait_ge(s_ident, 2)
            for j in range(2 * LAYERS + 2):
                nc.tensor.transpose(bank[5 + j // 4][:, D * (j % 4):D * (j % 4) + D], w_nat[:, j, :], ident[:, :])\
                    .then_inc(s_wTp, 1)
            pe.wait_ge(s_xlo, 2)
            pe.wait_ge(s_wT, 2)

            def chunk(it, c):
                n = CHUNKS * it + c
                pe.wait_ge(s_al, n + 1)
                for k in range(2):
                    if c == 0:
                        wait(pe, s_h0[k], it)
                    for m in range(CH):
                        b = CH * c + m
                        cols = slice(m * TILE, (m + 1) * TILE)
                        for j, (w, v) in enumerate(((xh[k], ah), (xl[k], ah), (xh[k], al))):
                            last = mm(acc[k][:, :], w[:, b, :], v[c % 2][:, cols], start=(b == 0 and j == 0),
                                      stop=(b == KB - 1 and j == 2))
                    if c == CHUNKS - 1:
                        last.then_inc(s_acc[k], 1)
                        if k == 1:
                            pe.wait_ge(s_acc[1], it + 1)
                            pe.sem_inc(s_used, 1)
                    elif k == 1:
                        last.then_inc(s_used, 1)

            def layer(it, l):
                for k in range(2):
                    if l == 0:
                        pe.wait_ge(s_h0[k], it + 1)
                    else:
                        pe.wait_ge(s_hid, 2 * (LAYERS * it + l - 1) + k + 1)
                    mm(lay[k][:, :], w_T[:, LAYERS * k + l, :], hid[k][l][:, :], start=True, stop=True).then_inc(s_lay, 1)

            def merge(it):
                pe.wait_ge(s_hid, 2 * LAYERS * (it + 1))
                wait(pe, s_ya, it)
                for q in range(RG):
                    for k in range(2):
                        last = mm(mrg[:, q, :], hid[k][LAYERS][:, P * q:P * q + P], w_T[:, 2 * LAYERS + k, :],
                                  start=(k == 0), stop=(k == 1))
                last.then_inc(s_mrg, 1)

            def stage_a(it, mlp):
                for c in range(CHUNKS):
                    chunk(it, c)
                    if mlp and c < LAYERS:
                        layer(it - 1, c)
                    if mlp and c == LAYERS:
                        merge(it - 1)

            stage_a(0, False)
            with pe.Fori(1, TILES) as it:
                stage_a(it, True)
            for l in range(LAYERS):
                layer(TILES - 1, l)
            merge(TILES - 1)

            pe.wait_ge(s_mrg, TILES)
            pe.sem_inc(s_aend, 1)
            pe.wait_ge(s_aend, 5)
            pe.wait_ge(b_xm, 16 * Q)
            pe.wait_ge(b_sel, 2)

            def adj_blocks(a, b0, b1):
                for b in range(b0, b1):
                    c, m = b // CH, b % CH
                    if m == 0:
                        pe.wait_ge(b_adj[c % NADJ], 16 * (CHUNKS // NADJ * a + c // NADJ + 1))
                    if b == 0:
                        wait(pe, b_ax, a)
                    last = mm(accB[:, :], xm[:, b, :], adjc[c % NADJ][:, m, :], start=(b == 0), stop=(b == KB - 1))
                    if b == KB - 1:
                        last.then_inc(b_acc, 1)
                        pe.wait_ge(b_acc, a + 1)
                        pe.sem_inc(b_adjused, 1)
                    elif m == CH - 1:
                        last.then_inc(b_adjused, 1)

            def front_gcn(a):
                pe.wait_ge(b_ax, a + 1)
                wait(pe, b_spab, 4 * a)
                for q in range(RG):
                    last = mm(M0g[:, q, :], axT[:, P * q:P * q + P], gcn_w_sb[:, :], start=True, stop=True)
                last.then_inc(b_gcn, 1)

            def front_tr(a):
                pe.wait_ge(b_hn, a + 1)
                for q in range(RG):
                    last = nc.tensor.transpose(M1[:, P * q:P * q + P], hn[:, q, :], ident[:, :])
                last.then_inc(b_tr, 1)

            def front_xc(a):
                pe.wait_ge(b_hT, a + 1)
                pe.wait_ge(b_g, a + 1)
                mm(M0[:, :], w_in_sb[:, 0:P], hT[:, :], start=True, stop=True)
                mm(M1[:, :], w_in_sb[:, P:2 * P], hT[:, :], start=True, stop=True).then_inc(b_xc, 1)

            def front_z(a):
                pe.wait_ge(b_xcev, 4 * a + 4)
                mm(M0[:, :], w_in_sb[:, 2 * P:3 * P], hT[:, :], start=True, stop=True)
                mm(M1[:, :], w_in_sb[:, 3 * P:4 * P], hT[:, :], start=True, stop=True).then_inc(b_z, 1)

            def front_dbc(a, par):
                pe.wait_ge(b_sz, 2 * a + 2)
                pe.wait_ge(b_u, a + 1)
                for h in range(H):
                    last = mm(M0[0:4 * S + R, :], w_xp_sb[:, h, :], u[par][:, h, :], start=(h == 0), stop=(h == 1))
                last.then_inc(b_dbc, 1)

            def front_dtp(a):
                pe.wait_ge(b_bc, a + 1)
                pe.wait_ge(b_bchi, 2 * a + 2)
                for h, m in enumerate((M1, M0)):
                    mm(m[:, :], w_dt_sb[64:64 + R, P * h:P * h + P], dtr[64:64 + R, :], start=True, stop=True)\
                        .then_inc(b_dtp, 1)

            def spread_B(b, n, par):
                if n == 0:
                    pe.wait_ge(b_bc, b + 1)
                k, bb = (n - 2, b) if n >= 2 else (n - 2 + S, b - 1)
                if not (isinstance(bb, int) and bb < 0):
                    if k in POOL_B:
                        pe.wait_ge(b_Bsb, NPB * bb + nB(k) + 1)
                    else:
                        pe.wait_ge(b_dbuV, NVB * bb + k - nB(k) + 1)
                mm(BB[n % 2][:, :], sel[0:4 * S, n, :], bc[par][0:4 * S, :], start=True, stop=True).then_inc(b_B, 1)

            def spread_C(b, n, par):
                wait(pe, b_p, S * b + n - 1)
                mm(CC[n % 2][:, :], sel[0:4 * S, S + n, :], bc[par][0:4 * S, :], start=True, stop=True).then_inc(b_C, 1)

            def tail_out(b, par):
                pe.wait_ge(b_yg, b + 1)
                wait(pe, b_os, b)
                for q in range(RG):
                    for h in range(H):
                        last = mm(O[:, q, :], y[par][:, h, P * q:P * q + P], w_out_sb[:, h, :], start=(h == 0), stop=(h == 1))
                last.then_inc(b_out, 1)

            def window(b, par, tail, front, adj_):
                spread_B(b, 0, par)
                for n in range(S):
                    if n + 1 < S:
                        spread_B(b, n + 1, par)
                    spread_C(b, n, par)
                    if front:
                        if n == 0:
                            front_gcn(b + 1)
                        if n == 3:
                            front_tr(b + 1)
                        if n == 4:
                            front_xc(b + 1)
                        if n == 5:
                            front_z(b + 1)
                        if n == 8:
                            front_dbc(b + 1, 1 - par)
                        if n == 10:
                            front_dtp(b + 1)
                    if tail and n == 4:
                        tail_out(b - 1, 1 - par)
                    if adj_:
                        adj_blocks(b + 2, 2 * n, 2 * n + 2)

            adj_blocks(0, 0, KB)
            front_gcn(0)
            adj_blocks(1, 0, 5)
            front_tr(0)
            adj_blocks(1, 5, 7)
            front_xc(0)
            front_z(0)
            adj_blocks(1, 7, 12)
            front_dbc(0, 0)
            adj_blocks(1, 12, 15)
            front_dtp(0)
            adj_blocks(1, 15, KB)
            window(0, 0, False, True, True)
            with pe.Fori(0, 2) as i:
                window(2 * i + 1, 1, True, True, True)
                window(2 * i + 2, 0, True, True, True)
            window(5, 1, True, True, True)
            window(6, 0, True, True, False)
            window(7, 1, True, False, False)
            tail_out(TILES - 1, 1)


_INS = ['x', 'adj', 'L0_gnn_x2', 'L0_gnn_eps1', 'L0_gnn_eps2', 'L0_gnn_W1', 'L0_gnn_b1', 'L0_gnn_W2', 'L0_gnn_b2',
        'L0_gnn_Wm', 'L0_gnn_bm', 'L1_gnn_gcn_w', 'L1_gnn_gcn_b', 'L1_gnn_ln_g', 'L1_gnn_ln_b', 'L1_gnn_w_in',
        'L1_gnn_conv_w', 'L1_gnn_conv_b', 'L1_gnn_w_xp', 'L1_gnn_w_dt', 'L1_gnn_b_dt', 'L1_gnn_A_log',
        'L1_gnn_D_skip', 'L1_gnn_w_out']


def kernel(**inputs):
    import numpy as np
    import concourse.bacc as bacc
    from concourse import mybir as _mybir
    from concourse.bass_utils import run_bass_kernel_spmd

    nc = bacc.Bacc("TRN2", target_bir_lowering=False, num_devices=1)
    arrays, args = {}, []
    for name in _INS:
        a = np.ascontiguousarray(inputs[name])
        arrays[f"in_{name}"] = a
        args.append(nc.dram_tensor(f"in_{name}", a.shape, _mybir.dt.from_np(a.dtype), kind="ExternalInput").ap())
    out = nc.dram_tensor("out", (4096, 128), _mybir.dt.float32, kind="ExternalOutput").ap()
    gnn_mamba(nc, *args, out)
    r = run_bass_kernel_spmd(nc, [arrays], core_ids=[0])
    return r.results[0]["out"]
```

```python
from contextlib import ExitStack

import concourse.bass as bass
from concourse import mybir

F32 = mybir.dt.float32
F32R = mybir.dt.float32r
ALU = mybir.AluOpType
ACT = mybir.ActivationFunctionType

P = 128
N = 4096
D = 128
TILE = 512
TILES = N // TILE
KB = N // P
CH = 4
CHUNKS = KB // CH
CHC = CH * TILE
Q = 4
GROUPS = TILE // 32
RG = TILE // P
LAYERS = 3
DI = 256
H = 2
S = 16
R = 8
TAPS = 4
EPS = 1e-5


def wait(eng, sem, value):
    if not isinstance(value, int) or value > 0:
        eng.wait_ge(sem, value)


AT = dict(pool_rs=2, pool_gate=3, pool_tail_rs=6, pool_dt=12, act_hn=5, act_hT=6, act_silu=9, act_bc=10,
          act_sp=12, act_exp=13, act_tail=9, dve_g=1, dve_bc=9, dve_sp=12, dve_y=3, dve_tail=6, pe_tr=3,
          pe_z=6, pe_dbc=8, pe_dt=9, pe_out=4, act_B=2, act_g=1, act_start=1, pe_C=0,
          pool_ahead=0)
FILL = (3, 6, 2, 0, 1, 2, 2, 16)
CONV = (0, 0, 0, 0, 4, 4, 0, 0, 0, 0, 0, 0, 0, 0, 0, 0)
PLAN = (2, 3, 3, 4, 0, 1, 1, 0, 1, 3, 3, 3, 2, 1, 3, 2)
POOL = (3, 6, 8, 11)


def gnn_mamba(nc, x, adj, x2, eps1, eps2, W1, b1, W2, b2, Wm, bm, gcn_w, gcn_b, ln_g, ln_b, w_in, conv_w,
              conv_b, w_xp, w_dt, b_dt, A_log, D_skip, w_out, out):
    POOL_B = POOL
    ctx = ExitStack()
    with ctx:
        def sem(name):
            return ctx.enter_context(nc.semaphore(name))

        def sb(name, shape, dt=F32, stack=ctx):
            return stack.enter_context(nc.sbuf_tensor(name, shape, dt))

        adjT = nc.dram_tensor("adjT", ((TILES - 1) * CHUNKS * P, CHC), F32, kind="Internal").ap()
        mid = nc.dram_tensor("mid", (N, D), F32, kind="Internal").ap()

        ident = sb("ident", [P, P])
        neg_half = sb("neg_half", [P, RG])
        eps_ln = sb("eps_ln", [P, RG])
        zero = sb("zero", [P, 1])
        ones = sb("ones", [P, P])
        neg_one = sb("neg_one", [P, RG])
        gcn_w_sb = sb("gcn_w_sb", [P, D])
        gcn_b_sb = sb("gcn_b_sb", [P, D])
        bm_sb = sb("bm_sb", [P, D])
        ln_g_sb = sb("ln_g_sb", [P, 1])
        ln_b_sb = sb("ln_b_sb", [P, 1])
        w_in_sb = sb("w_in_sb", [P, 2 * DI])
        conv_w_sb = sb("conv_w_sb", [P, H, TAPS])
        conv_b_sb = sb("conv_b_sb", [P, H])
        w_xp_sb = sb("w_xp_sb", [P, H, P])
        w_dt_sb = sb("w_dt_sb", [P, DI])
        w_cv_sb = sb("w_cv_sb", [P, H, TAPS, P])
        b_dt_sb = sb("b_dt_sb", [P, H])
        A_sb = sb("A_sb", [P, H, S])
        D_sb = sb("D_sb", [P, H])
        w_out_sb = sb("w_out_sb", [P, H, D])
        eps_sb = sb("eps_sb", [P, 2])
        bias_sb = sb("bias_sb", [P, 2, LAYERS])
        stats = sb("stats", [P, RG, 6])
        stat_in = sb("stat_in", [P, 1])
        mv = sb("mv", [P, RG, 2])
        ve = sb("ve", [P, RG])
        rs = sb("rs", [P, RG])
        mr = sb("mr", [P, RG])
        nb = sb("nb", [P, RG])
        stats2 = sb("stats2", [P, RG, 6])
        mv2 = sb("mv2", [P, RG, 2])
        ve2 = sb("ve2", [P, RG])
        rs2 = sb("rs2", [P, RG])
        mr2 = sb("mr2", [P, RG])
        nb2 = sb("nb2", [P, RG])
        res = [sb(f"res{i}", [P, RG, D]) for i in range(2)]
        state = sb("state", [P, S, H])
        xm = sb("xm", [P, KB, D])

        A = ExitStack()
        xh = [sb(f"xh{k}", [P, KB, D], F32R, A) for k in range(2)]
        xl = [sb(f"xl{k}", [P, KB, D], F32R, A) for k in range(2)]
        ah = [sb(f"ah{k}", [P, CHC], F32R, A) for k in range(2)]
        al = [sb(f"al{k}", [P, CHC], F32R, A) for k in range(2)]
        NROWS = 4
        rows = [sb(f"rows{k}", [P, GROUPS, P], F32, A) for k in range(NROWS)]
        at = [sb(f"at{k}", [P, CH, TILE], F32, A) for k in range(2)]
        w_nat = sb("w_nat", [P, 2 * LAYERS + 2, D], F32, A)
        w_T = sb("w_T", [P, 2 * LAYERS + 2, D], F32, A)
        A1 = ExitStack()
        xs = [xm, sb("xs1", [P, KB, D], F32, A1)]
        A1.close()
        hid = [[sb(f"hid{k}_{l}", [P, TILE], F32, A) for l in range(LAYERS + 1)] for k in range(2)]
        ysum = sb("ysum", [P, RG, D], F32, A)
        xn = sb("xn", [P, RG, D], F32, A)
        A.close()

        B = ExitStack()
        NADJ = 4
        adjc = [sb(f"adjc{k}", [P, CH, TILE], F32, B) for k in range(NADJ)]
        sel = sb("sel", [P, 2 * S, P], F32R, B)
        w_dth = sb("w_dth", [P, DI], F32R, B)
        w_dtl = sb("w_dtl", [P, DI], F32R, B)
        axT = sb("axT", [P, TILE], F32, B)
        g = sb("g", [P, RG, D], F32, B)
        hn = sb("hn", [P, RG, D], F32, B)
        hT = sb("hT", [P, TAPS - 1 + TILE], F32, B)
        u = [sb(f"u{k}", [P, H, TILE], F32, B) for k in range(2)]
        sz = [sb(f"sz{k}", [P, H, TILE], F32, B) for k in range(2)]
        sp_a = sb("sp_a", [P, H, TILE], F32, B)
        sp_r = sb("sp_r", [P, H, TILE], F32, B)
        dt_ = [sb(f"dt{k}", [P, H, TILE], F32, B) for k in range(2)]
        dtu = [sb(f"dtu{k}", [P, H, TILE], F32, B) for k in range(2)]
        bc = [sb(f"bc{k}", [P, TILE], F32R, B) for k in range(2)]
        NDA, NPR = 4, 4
        dA = [sb(f"dA{k}", [P, H, 1 + TILE], F32, B) for k in range(NDA)]
        dBuV = [sb(f"dBuV{k}", [P, H, 1 + TILE], F32, B) for k in range(2)]
        dBuP = [sb(f"dBuP{k}", [P, H, 1 + TILE], F32, B) for k in range(2)]
        hs = [sb(f"hs{k}", [P, H, 1 + TILE], F32, B) for k in range(2)]
        pr = [sb(f"pr{k}", [P, H, TILE], F32, B) for k in range(NPR)]
        y = [sb(f"y{k}", [P, H, TILE], F32, B) for k in range(2)]
        b_sb = [sb(f"b_sb{k}", [P, TILE], F32, B) for k in range(2)]
        o_n = sb("o_n", [P, RG, D], F32, B)
        B.close()

        bank = [ctx.enter_context(nc.psum_tensor(f"bank{i}", [P, TILE], F32)) for i in range(8)]
        acc = [bank[0], bank[1]]
        lay = [bank[2], bank[3]]
        mrg = bank[4][:, :].rearrange("p (g d) -> p g d", g=RG)
        accB, M0, M1 = bank[7], bank[1], bank[2]
        BB = [bank[3], bank[5]]
        CC = [bank[4], bank[6]]
        O = bank[0][:, :].rearrange("p (g d) -> p g d", g=RG)
        M0g = M0[:, :].rearrange("p (g d) -> p g d", g=RG)

        s_w = sem("s_w")
        s_ident = sem("s_ident")
        XP = 4
        s_xload = [sem(f"s_xload{k}") for k in range(2 * XP)]
        s_xhi, s_xlo = sem("s_xhi"), sem("s_xlo")
        s_wTp, s_wT = sem("s_wTp"), sem("s_wT")
        s_rows = [sem(f"s_rows{k}") for k in range(NROWS)]
        s_at = sem("s_at")
        s_atout = [sem(f"s_atout{k}") for k in range(2)]
        s_ah, s_al = sem("s_ah"), sem("s_al")
        s_used = sem("s_used")
        s_acc = [sem(f"s_acc{k}") for k in range(2)]
        s_h0 = [sem(f"s_h0{k}") for k in range(2)]
        s_lay, s_hid = sem("s_lay"), sem("s_hid")
        s_mrg, s_ya, s_yb, s_st, s_mv = sem("s_mrg"), sem("s_ya"), sem("s_yb"), sem("s_st"), sem("s_mv")
        s_ve, s_rs, s_xn, s_mid = sem("s_ve"), sem("s_rs"), sem("s_xn"), sem("s_mid")
        s_res = sem("s_res")
        b_res = [sem(f"b_res{k}") for k in range(2)]
        s_prepA = sem("s_prepA")
        s_aend = sem("s_aend")

        b_xm = sem("b_xm")
        b_adj = [sem(f"b_adj{k}") for k in range(NADJ)]
        b_adjused, b_acc, b_ax = sem("b_adjused"), sem("b_acc"), sem("b_ax")
        b_gcn, b_g, b_st, b_mv, b_ve, b_rs, b_hn = [sem(f"b_{n}") for n in "gcn g st mv ve rs hn".split()]
        b_tr, b_hT, b_xc, b_hist = [sem(f"b_{n}") for n in "tr hT xc hist".split()]
        b_z, b_u, b_sz, b_dbc, b_bchi, b_bc, b_dtp = [sem(f"b_{n}") for n in "z u sz dbc bchi bc dtp".split()]
        b_spab, b_spe, b_spw, b_spl, b_spd, b_sps, b_dtv, b_dtu = [sem(f"b_{n}") for n in "spab spe spw spl spd sps dtv dtu".split()]
        b_B, b_C, b_Bsb, b_dA = [sem(f"b_{n}") for n in "B C Bsb dA".split()]
        b_dbuV, b_dbuP, b_scan, b_state, b_p, b_y = [sem(f"b_{n}") for n in "dbuV dbuP scan state p y".split()]
        b_yd, b_yg, b_out, b_ost, b_omv, b_ove, b_ors, b_on = [sem(f"b_{n}") for n in "yd yg out ost omv ove ors on".split()]
        b_store = sem("b_store")
        b_zero, b_start = sem("b_zero"), sem("b_start")
        b_sel, b_wdt = sem("b_sel"), sem("b_wdt")
        b_mr, b_nb, b_omr, b_onb = sem("b_mr"), sem("b_nb"), sem("b_omr"), sem("b_onb")
        s_wcp, s_wcs, s_wcq, s_wc = sem("s_wcp"), sem("s_wcs"), sem("s_wcq"), sem("s_wc")

        WLOADS = 32
        XB = KB // XP

        def nB(n):
            return sum(1 for k in POOL_B if k < n)

        NPB = len(POOL_B)
        NVB = S - NPB

        def v_slot(n, par):
            return (n - nB(n) + NVB * par) % 2

        def b_slot(n, par):
            return (nB(n) + NPB * par) % 2

        def dBu(n, par):
            return dBuP[b_slot(n, par)] if n in POOL_B else dBuV[v_slot(n, par)]

        def stage_a_over(eng):
            eng.wait_ge(s_aend, 3)
            eng.wait_ge(b_acc, 1)

        block = ctx.enter_context(nc.Block())

        def load_rows(eng, quads, it, c):
            for q in quads:
                src = adj[bass.ds(it * TILE, TILE), TILE * c + P * q:TILE * c + P * q + P].rearrange("(g i) c -> i g c", g=GROUPS)
                eng.dma_start(rows[c % NROWS][32 * q:32 * q + 32, :, :], src).then_inc(s_rows[c % NROWS], 16)

        @block.sync
        def _(sp):
            def load_x(part):
                tiles = slice(XB // CH * part, XB // CH * (part + 1))
                for k, src in enumerate((x, x2)):
                    sp.dma_start(xs[k][:, XB * part:XB * (part + 1), :].rearrange("p (t m) d -> p t (m d)", m=CH),
                                 src.rearrange("(t p m) d -> p t (m d)", p=P, m=CH)[:, tiles])\
                        .then_inc(s_xload[2 * part + k], 16)

            load_rows(sp, (0, 1), 0, 0)
            load_x(0)
            for c in range(1, NROWS):
                load_rows(sp, (0, 1), 0, c)
                load_x(c)

            def stage_a(it, store):
                for c in range(CHUNKS):
                    sp.wait_ge(s_at, CHUNKS * it + c + 1)
                    if store:
                        sp.dma_start(adjT[bass.ds(((it - 1) * CHUNKS + c) * P, P), :],
                                     at[c % 2][:, :, :].rearrange("p m t -> p (m t)")).then_inc(s_atout[c % 2], 16)
                    after = it + (c + NROWS) // CHUNKS
                    load_rows(sp, (0, 1), 0 if isinstance(after, int) and after == TILES else after, (c + NROWS) % CHUNKS)

            stage_a(0, False)
            for k in range(2):
                sp.sem_inc(s_atout[k], 16)
            with sp.Fori(1, TILES - 1) as it:
                stage_a(it, True)
            stage_a(TILES - 1, True)
            for k in range(2):
                sp.wait_ge(s_atout[k], 16 * ((TILES - 1) * CHUNKS // 2 + 1))
            sp.sem_inc(s_aend, 1)
            sp.wait_ge(s_used, TILES * CHUNKS)
            for c in range(NROWS, CHUNKS):
                sp.wait_ge(s_at, CHUNKS * TILES + c - NROWS + 1)
                load_rows(sp, range(Q), 0, c)

            def load_adj(a, chunks):
                for c in chunks:
                    wait(sp, b_adjused, CHUNKS * (a - 1) + c - NADJ + 1)
                    sp.dma_start(adjc[c % NADJ][:, :, :].rearrange("p m t -> p (m t)"),
                                 adjT[bass.ds(((a - 1) * CHUNKS + c) * P, P), :]).then_inc(b_adj[c % NADJ], 16)

            def load_res(b, par):
                wait(sp, b_out, b - 1)
                sp.dma_start(res[par][:, :, :], mid[bass.ds(b * TILE, TILE), :].rearrange("(g p) d -> p g d", g=RG))\
                    .then_inc(b_res[par], 16)

            def store(b):
                sp.wait_ge(b_on, RG * (b + 1))
                sp.dma_start(out[bass.ds(b * TILE, TILE), :].rearrange("(g p) d -> p g d", g=RG), o_n[:, :, :])\
                    .then_inc(b_store, 16)

            def window(b, par, tail, adj_):
                load_res(b, par)
                if adj_:
                    load_adj(b + 2, range(0, CHUNKS - 2))
                if tail:
                    store(b - 1)
                if adj_:
                    load_adj(b + 2, range(CHUNKS - 2, CHUNKS))

            load_adj(1, range(CHUNKS))
            window(0, 0, False, True)
            window(1, 1, True, True)
            with sp.Fori(0, 2) as i:
                window(2 * i + 2, 0, True, True)
                window(2 * i + 3, 1, True, True)
            window(6, 0, True, False)
            window(7, 1, True, False)
            store(TILES - 1)
            sp.wait_ge(b_store, 16 * TILES)

        @block.gpsimd
        def _(pool):
            nc.gpsimd.memset(w_xp_sb[:, :, :], 0.0).then_inc(s_ident, 1)
            nc.gpsimd.memset(w_dt_sb[:, :], 0.0).then_inc(s_ident, 1)
            pool.wait_ge(s_ident, 2)
            loads = []

            def load(dst, src):
                loads.append(dst)
                pool.dma_start(dst, src).then_inc(s_w, 16)

            for k in range(2):
                pool.wait_ge(s_xload[k], 16)
            load(w_nat[:, 0:LAYERS, :], W1.rearrange("l o d -> o l d"))
            load(w_nat[:, LAYERS:2 * LAYERS, :], W2.rearrange("l o d -> o l d"))
            load(w_nat[:, 2 * LAYERS:, :].rearrange("p k d -> p (k d)"), Wm)
            for k, b in enumerate((b1, b2)):
                for l in range(LAYERS):
                    load(bias_sb[:, k, l:l + 1], b[l].rearrange("(p o) -> p o", o=1))
            load(eps_sb[:, 0:1], eps1.partition_broadcast(P))
            load(eps_sb[:, 1:2], eps2.partition_broadcast(P))
            load(bm_sb[:, :], bm.partition_broadcast(P))
            load(gcn_b_sb[:, :], gcn_b.partition_broadcast(P))
            load(gcn_w_sb[:, :], gcn_w)
            load(ln_g_sb[:, :], ln_g.rearrange("(p o) -> p o", o=1))
            load(ln_b_sb[:, :], ln_b.rearrange("(p o) -> p o", o=1))
            load(w_in_sb[:, :], w_in)
            load(conv_w_sb[:, :, :], conv_w.rearrange("(h p) k -> p h k", h=H))
            for at_ in (2 * S, 6 * S):
                load(w_dt_sb[at_:at_ + R, :], w_dt)
            load(A_sb[:, :, :], A_log.rearrange("(h p) s -> p h s", h=H))
            load(w_out_sb[:, :, :], w_out.rearrange("(h p) d -> p h d", h=H))
            for h in range(H):
                for dst, src in ((conv_b_sb, conv_b), (b_dt_sb, b_dt), (D_sb, D_skip)):
                    load(dst[:, h:h + 1], src.rearrange("(h p o) -> h p o", h=H, o=1)[h])
            v = w_xp.rearrange("(h p) j -> p h j", h=H)
            for half in range(2):
                load(w_xp_sb[:, :, 4 * S * half:4 * S * half + 2 * S], v[:, :, R:])
                load(w_xp_sb[:, :, 4 * S * half + 2 * S:4 * S * half + 2 * S + R], v[:, :, 0:R])
            assert len(loads) == WLOADS, len(loads)

            nc.gpsimd.memset(ident[:, :], 0.0).then_inc(s_ident, 1)
            pool.wait_ge(s_ident, 3)
            nc.gpsimd.affine_select(out=ident[:, :], in_=ident[:, :], compare_op=ALU.not_equal, fill=1.0, base=0,
                                    pattern=[[-1, P]], channel_multiplier=1).then_inc(s_ident, 1)
            nc.gpsimd.memset(neg_half[:, :], -0.5).then_inc(s_ident, 1)
            nc.gpsimd.memset(eps_ln[:, :], EPS).then_inc(s_ident, 1)
            nc.gpsimd.memset(neg_one[:, :], -1.0).then_inc(s_ident, 1)
            nc.gpsimd.memset(zero[:, :], 0.0).then_inc(s_ident, 1)
            nc.gpsimd.memset(ones[:, :], 1.0).then_inc(s_ident, 1)
            pool.wait_ge(s_ident, 9)

            def load_res(it, par):
                pool.dma_start(res[par][:, :, :], x[bass.ds(it * TILE, TILE), :].rearrange("(g p) d -> p g d", g=RG))\
                    .then_inc(s_res, 16)

            def norm(it):
                pool.wait_ge(s_mv, it + 1)
                nc.gpsimd.tensor_tensor(ve[:, :], mv[:, :, 1], eps_ln[:, :], ALU.add).then_inc(s_ve, 1)
                pool.wait_ge(s_ve, it + 1)
                nc.gpsimd.tensor_tensor(rs[:, :], ve[:, :], neg_half[:, :], ALU.pow).then_inc(s_rs, 1)
                pool.wait_ge(s_xn, it + 1)
                pool.dma_start(mid[bass.ds(it * TILE, TILE), :].rearrange("(g p) d -> p g d", g=RG), xn[:, :, :])\
                    .then_inc(s_mid, 16)
                pool.wait_ge(s_mid, 16 * it + 16)
                pool.dma_start(xm[:, bass.ds(it * CH, CH), :].rearrange("p m d -> p (m d)"),
                               mid[bass.ds(it * TILE, TILE), :].rearrange("(p m) d -> p (m d)", m=CH)).then_inc(b_xm, 16)

            load_res(0, 0)
            with pool.Fori(0, TILES - 1) as it:
                norm(it)
                load_res(it + 1, 0)
            pool.wait_ge(s_used, TILES * CHUNKS)
            nc.gpsimd.memset(state[:, :, :], 0.0).then_inc(b_zero, 1)
            nc.gpsimd.memset(hT[:, :], 0.0).then_inc(b_zero, 1)
            norm(TILES - 1)
            pool.wait_ge(b_xm, 16 * TILES)
            pool.sem_inc(s_aend, 1)


            def front_rs(a):
                pool.wait_ge(b_mv, a + 1)
                nc.gpsimd.tensor_tensor(ve[:, :], mv[:, :, 1], eps_ln[:, :], ALU.add).then_inc(b_ve, 1)
                pool.wait_ge(b_ve, a + 1)
                nc.gpsimd.tensor_tensor(rs[:, :], ve[:, :], neg_half[:, :], ALU.pow).then_inc(b_rs, 1)
                pool.wait_ge(b_rs, a + 1)
                nc.gpsimd.tensor_tensor(mr[:, :], mv[:, :, 0], rs[:, :], ALU.mult).then_inc(b_mr, 1)
                pool.wait_ge(b_mr, a + 1)
                nc.gpsimd.tensor_tensor(nb[:, :], mr[:, :], neg_one[:, :], ALU.mult).then_inc(b_nb, 1)

            def front_dt(a, par, step):
                if step == 0:
                    pool.wait_ge(b_spd, a + 1)
                    nc.gpsimd.tensor_tensor(dt_[par][:, :, :], dt_[par][:, :, :], sp_a[:, :, :], ALU.subtract)\
                        .then_inc(b_sps, 1)
                elif step == 1:
                    pool.wait_ge(b_sps, a + 1)
                    nc.gpsimd.tensor_tensor(dt_[par][:, :, :], dt_[par][:, :, :], sp_r[:, :, :], ALU.add).then_inc(b_dtv, 1)
                else:
                    pool.wait_ge(b_dtv, a + 1)
                    nc.gpsimd.tensor_tensor(dtu[par][:, :, :], dt_[par][:, :, :], u[par][:, :, :], ALU.mult)\
                        .then_inc(b_dtu, 1)

            def tail_gate(b, par):
                pool.wait_ge(b_yd, b + 1)
                nc.gpsimd.tensor_tensor(y[par][:, :, :], y[par][:, :, :], sz[par][:, :, :], ALU.mult).then_inc(b_yg, 1)

            def tail_rs(b):
                pool.wait_ge(b_omv, b + 1)
                nc.gpsimd.tensor_tensor(ve2[:, :], mv2[:, :, 1], eps_ln[:, :], ALU.add).then_inc(b_ove, 1)
                pool.wait_ge(b_ove, b + 1)
                nc.gpsimd.tensor_tensor(rs2[:, :], ve2[:, :], neg_half[:, :], ALU.pow).then_inc(b_ors, 1)
                pool.wait_ge(b_ors, b + 1)
                nc.gpsimd.tensor_tensor(mr2[:, :], mv2[:, :, 0], rs2[:, :], ALU.mult).then_inc(b_omr, 1)
                pool.wait_ge(b_omr, b + 1)
                nc.gpsimd.tensor_tensor(nb2[:, :], mr2[:, :], neg_one[:, :], ALU.mult).then_inc(b_onb, 1)

            def window(b, par, tail, front):
                for step in range(S + 2):
                    n = step + AT['pool_ahead']
                    if n in POOL_B:
                        pool.wait_ge(b_Bsb, NPB * b + nB(n) + 1)
                        before = [j for j in range(-S, n) if j % S in POOL_B][-2]
                        wait(pool, b_scan, S * b + before + 1)
                        pool.wait_ge(b_dtu, b + 1)
                        nc.gpsimd.tensor_tensor(dBu(n, par)[:, :, 1:], dtu[par][:, :, :],
                                                b_sb[b_slot(n, par)][:, :].unsqueeze(1).to_broadcast([P, H, TILE]),
                                                ALU.mult).then_inc(b_dbuP, 1)
                    n = step
                    k = n - 2
                    if k == 1:
                        wait(pool, b_out, b - 1)
                        pool.wait_ge(b_p, S * b + 2)
                        nc.gpsimd.tensor_tensor(y[par][:, :, :], pr[0][:, :, :], pr[1][:, :, :], ALU.add).then_inc(b_y, 1)
                    elif k > 1:
                        pool.wait_ge(b_p, S * b + k + 1)
                        pool.wait_ge(b_y, (S - 1) * b + k - 1)
                        nc.gpsimd.tensor_tensor(y[par][:, :, :], y[par][:, :, :], pr[k % NPR][:, :, :], ALU.add).then_inc(b_y, 1)
                    if front and n == AT['pool_rs']:
                        front_rs(b + 1)
                    if tail and n == AT['pool_gate']:
                        tail_gate(b - 1, 1 - par)
                    if tail and n == AT['pool_tail_rs']:
                        tail_rs(b - 1)
                    if front and 0 <= n - AT['pool_dt'] < 3:
                        front_dt(b + 1, 1 - par, n - AT['pool_dt'])

            front_rs(0)
            stage_a_over(pool)
            for a in dA:
                nc.gpsimd.memset(a[:, :, 0:1], 0.0).then_inc(b_zero, 1)
            for step in range(3):
                front_dt(0, 0, step)
            window(0, 0, False, True)
            window(1, 1, True, True)
            with pool.Fori(0, 2) as i:
                window(2 * i + 2, 0, True, True)
                window(2 * i + 3, 1, True, True)
            window(6, 0, True, True)
            window(7, 1, True, False)
            tail_gate(TILES - 1, 1)
            tail_rs(TILES - 1)

        @block.scalar
        def _(act):
            for c in range(NROWS):
                load_rows(act, (2, 3), 0, c)
            act.preload_act_table_set("natural_log_exp_and_others")

            def x_hi(part):
                blocks = slice(XB * part, XB * (part + 1))
                for k in range(2):
                    act.wait_ge(s_xload[2 * part + k], 16)
                    nc.scalar.activation(xh[k][:, blocks, :], xs[k][:, blocks, :], ACT.Copy).then_inc(s_xhi, 1)

            def hi(it, c):
                n = CHUNKS * it + c
                act.wait_ge(s_at, n + 1)
                wait(act, s_used, n - 1)
                nc.scalar.activation(ah[c % 2][:, :], at[c % 2][:, :, :].rearrange("p m t -> p (m t)"), ACT.Copy)\
                    .then_inc(s_ah, 1)

            def first(it):
                for k in range(2):
                    act.wait_ge(s_acc[k], it + 1)
                    nc.scalar.activation(hid[k][0][:, :], acc[k][:, :], ACT.Identity, scale=eps_sb[:, k:k + 1])\
                        .then_inc(s_h0[k], 1)

            def layer(it, l):
                for k in range(2):
                    act.wait_ge(s_lay, 2 * (LAYERS * it + l) + k + 1)
                    nc.scalar.activation(hid[k][l + 1][:, :], lay[k][:, :], ACT.Relu, bias=bias_sb[:, k, l:l + 1])\
                        .then_inc(s_hid, 1)

            def stage_a(it, mlp):
                for c in range(CHUNKS):
                    hi(it, c)
                    if not mlp and c in (0, 2, 4):
                        x_hi(c // 2 + 1)
                    after = it + (c + NROWS) // CHUNKS
                    load_rows(act, (2, 3), 0 if isinstance(after, int) and after == TILES else after, (c + NROWS) % CHUNKS)
                    if mlp and c == 0:
                        first(it - 1)
                    if mlp and c in (2, 3, 4):
                        layer(it - 1, c - 2)

            x_hi(0)
            stage_a(0, False)
            act.wait_ge(s_w, 16 * WLOADS)
            nc.scalar.activation(eps_sb[:, :], eps_sb[:, :], ACT.Identity, bias=2.0).then_inc(s_prepA, 1)
            act.wait_ge(s_prepA, 1)
            act.wait_ge(s_wcp, H)
            act.wait_ge(s_wTp, 8)
            for h in range(H):
                for k in range(TAPS):
                    nc.scalar.activation(w_nat[:, TAPS * h + k, :], bank[7][:, P * h:P * h + P], ACT.Copy,
                                         scale=conv_w_sb[:, h, k:k + 1]).then_inc(s_wcs, 1)
            with act.Fori(1, TILES - 1) as it:
                stage_a(it, True)
            stage_a(TILES - 1, True)
            first(TILES - 1)
            for l in range(LAYERS):
                layer(TILES - 1, l)

            act.preload_act_table_set("natural_log_exp_and_others")
            nc.scalar.activation(A_sb[:, :, :], A_sb[:, :, :], ACT.Exp).then_inc(s_prepA, 1)
            act.wait_ge(s_prepA, 2)
            nc.scalar.activation(A_sb[:, :, :], A_sb[:, :, :], ACT.Copy, scale=-1.0).then_inc(s_prepA, 1)
            act.wait_ge(s_prepA, 3)
            act.wait_ge(b_zero, 2)
            act.wait_ge(s_used, TILES * CHUNKS)
            act.wait_ge(s_ident, 9)
            for at_ in (0, 4 * S):
                for blk in (slice(at_, at_ + 32), slice(at_ + 32, at_ + 64)):
                    nc.scalar.activation(sel[blk, :, :], ident[blk, at_:at_ + 32].unsqueeze(2).to_broadcast([32, 2 * S, P]),
                                         ACT.Copy).then_inc(b_sel, 1)
            nc.scalar.activation(w_dth[:, :], w_dt_sb[:, :], ACT.Copy).then_inc(b_wdt, 1)

            def front_ax(a):
                act.wait_ge(b_acc, a + 1)
                wait(act, b_gcn, a)
                nc.scalar.activation(axT[:, :], accB[:, :], ACT.Copy).then_inc(b_ax, 1)

            def front_relu(a):
                act.wait_ge(b_gcn, a + 1)
                wait(act, b_hn, RG * a)
                nc.scalar.activation(g[:, :, :], M0g, ACT.Relu).then_inc(b_g, 1)

            def front_hn(a):
                act.wait_ge(b_nb, a + 1)
                wait(act, b_tr, a)
                for q in range(RG):
                    nc.scalar.activation(hn[:, q, :], g[:, q, :], ACT.Identity, bias=nb[:, q:q + 1],
                                         scale=rs[:, q:q + 1]).then_inc(b_hn, 1)

            def front_hT(a):
                act.wait_ge(b_tr, a + 1)
                wait(act, b_z, H * a)
                nc.scalar.activation(hT[:, 0:TAPS - 1], hT[:, TILE:TILE + TAPS - 1], ACT.Copy).then_inc(b_hist, 1)
                act.wait_ge(b_hist, a + 1)
                nc.scalar.activation(hT[:, TAPS - 1:], M1[:, :], ACT.Identity, bias=ln_b_sb[:, :], scale=ln_g_sb[:, :])\
                    .then_inc(b_hT, 1)

            def front_silu(a, par):
                wait(act, b_yd, a - 1)
                wait(act, b_yg, a - 1)
                for h, m in enumerate((M0, M1)):
                    act.wait_ge(b_xc, H * a + h + 1)
                    nc.scalar.activation(u[par][:, h, :], m[:, :], ACT.Silu, bias=conv_b_sb[:, h:h + 1]).then_inc(b_u, 1)
                for h, m in enumerate((M0, M1)):
                    act.wait_ge(b_z, H * a + h + 1)
                    nc.scalar.activation(sz[par][:, h, :], m[:, :], ACT.Silu).then_inc(b_sz, 1)
                act.preload_act_table_set("natural_log_exp_and_others")

            def front_bc(a, par):
                act.wait_ge(b_dbc, a + 1)
                wait(act, b_C, S * (a - 1))
                nc.scalar.activation(bc[par][:, :], M0[:, :], ACT.Copy).then_inc(b_bchi, 1)

            def front_sp(a, par, step):
                if step == 0:
                    act.wait_ge(b_dtp, H * (a + 1))
                    wait(act, b_dtv, a)
                    for h, m in enumerate((M1, M0)):
                        nc.scalar.activation(sp_a[:, h, :], m[:, :], ACT.Abs, bias=b_dt_sb[:, h:h + 1]).then_inc(b_spab, 1)
                        nc.scalar.activation(sp_r[:, h, :], m[:, :], ACT.Relu, bias=b_dt_sb[:, h:h + 1]).then_inc(b_spab, 1)
                else:
                    act.wait_ge(b_spab, 4 * a + 4)
                    nc.scalar.activation(sp_a[:, :, :], sp_a[:, :, :], ACT.Exp, scale=-1.0).then_inc(b_spe, 1)
                    act.wait_ge(b_spe, a + 1)
                    nc.scalar.activation(dtu[par][:, :, :], sp_a[:, :, :], ACT.Identity, bias=1.0).then_inc(b_spw, 1)
                    act.wait_ge(b_spw, a + 1)
                    nc.scalar.activation(dt_[par][:, :, :], dtu[par][:, :, :], ACT.Ln).then_inc(b_spl, 1)

            def window(b, par, tail, front):
                for n in range(S + NDA):
                    k = n - NDA
                    if k >= 0:
                        act.wait_ge(b_scan, S * b + k + 1)
                        nc.scalar.activation(state[:, k, :], hs[k % 2][:, :, TILE], ACT.Copy).then_inc(b_state, 1)
                    if n < S:
                        if n == 0:
                            act.wait_ge(b_dtv, b + 1)
                        wait(act, b_scan, S * b + n - NDA + 1)
                        for h in range(H):
                            nc.scalar.activation(dA[n % NDA][:, h, 1:], dt_[par][:, h, :], ACT.Exp,
                                                 scale=A_sb[:, h, n:n + 1]).then_inc(b_dA, 1)
                    k = n - AT['act_start']
                    if 0 <= k < S:
                        same = [j for j in range(-S, k) if (j % S in POOL_B) == (k in POOL_B)]
                        wait(act, b_scan, S * b + same[-2] + 1)
                        wait(act, b_state, S * (b - 1) + k + 1)
                        nc.scalar.activation(dBu(k, par)[:, :, 0], state[:, k, :], ACT.Copy).then_inc(b_start, 1)
                    k = n - AT['act_B']
                    if k in POOL_B:
                        act.wait_ge(b_B, S * b + k + 1)
                        wait(act, b_dbuP, NPB * b + nB(k) - 1)
                        nc.scalar.activation(b_sb[(nB(k) + NPB * par) % 2][:, :], BB[k % 2][:, :], ACT.Copy).then_inc(b_Bsb, 1)
                    if front:
                        if n == 0:
                            front_ax(b + 1)
                        if n == AT['act_g']:
                            front_relu(b + 1)
                        if n == AT['act_hn']:
                            front_hn(b + 1)
                        if n == AT['act_hT']:
                            front_hT(b + 1)
                        if n == AT['act_silu']:
                            front_silu(b + 1, 1 - par)
                        if n == AT['act_bc']:
                            front_bc(b + 1, 1 - par)
                        if n == AT['act_sp']:
                            front_sp(b + 1, 1 - par, 0)
                        if n == AT['act_exp']:
                            front_sp(b + 1, 1 - par, 1)
                    if tail and n == AT['act_tail']:
                        tail_norm(b - 1)

            def tail_norm(b):
                act.wait_ge(b_onb, b + 1)
                wait(act, b_store, 16 * b)
                for q in range(RG):
                    nc.scalar.activation(o_n[:, q, :], O[:, q, :], ACT.Identity, bias=nb2[:, q:q + 1],
                                         scale=rs2[:, q:q + 1]).then_inc(b_on, 1)

            front_ax(0)
            front_relu(0)
            front_hn(0)
            front_hT(0)
            stage_a_over(act)
            front_silu(0, 0)
            front_bc(0, 0)
            front_sp(0, 0, 0)
            front_sp(0, 0, 1)
            window(0, 0, False, True)
            window(1, 1, True, True)
            with act.Fori(0, 2) as i:
                window(2 * i + 2, 0, True, True)
                window(2 * i + 3, 1, True, True)
            window(6, 0, True, True)
            window(7, 1, True, False)
            tail_norm(TILES - 1)

        @block.vector
        def _(dve):
            def x_lo(part):
                blocks = slice(XB * part, XB * (part + 1))
                for k in range(2):
                    dve.wait_ge(s_xhi, 2 * part + k + 1)
                    nc.vector.tensor_tensor(xl[k][:, blocks, :], xs[k][:, blocks, :], xh[k][:, blocks, :], ALU.subtract)\
                        .then_inc(s_xlo, 1)

            def transpose(it, c):
                n = CHUNKS * it + c
                dve.wait_ge(s_rows[c % NROWS], 16 * Q * (CHUNKS // NROWS * it + c // NROWS + 1))
                if isinstance(it, int) and it == TILES and c >= 2:
                    dve.wait_ge(s_used, n - 1)
                else:
                    wait(dve, s_al, n - 1)
                    if not (isinstance(it, int) and it == 0):
                        dve.wait_ge(s_atout[c % 2], 16 * (CHUNKS // 2 * (it - 1) + c // 2 + 1))
                half = GROUPS // 2
                for j in range(2):
                    src = rows[c % NROWS][:, half * j:half * j + half, :]
                    dst = at[c % 2][:, :, 32 * half * j:32 * half * (j + 1)]
                    last = nc.vector.transpose(dst.rearrange("p m (g i) -> p g m i", i=32),
                                               src.rearrange("p g (i m) -> p g m i", i=32))
                last.then_inc(s_at, 1)

            def lo(it, c):
                n = CHUNKS * it + c
                dve.wait_ge(s_ah, n + 1)
                wait(dve, s_used, n - 1)
                nc.vector.tensor_tensor(al[c % 2][:, :], at[c % 2][:, :, :].rearrange("p m t -> p (m t)"),
                                        ah[c % 2][:, :], ALU.subtract).then_inc(s_al, 1)

            def norm_stats(it):
                dve.wait_ge(s_mrg, it + 1)
                nc.vector.tensor_tensor(ysum[:, :, :], mrg, bm_sb[:, :].unsqueeze(1).to_broadcast([P, RG, D]), ALU.add)\
                    .then_inc(s_ya, 1)
                dve.wait_ge(s_ya, it + 1)
                dve.wait_ge(s_res, 16 * it + 16)
                nc.vector.tensor_tensor(ysum[:, :, :], ysum[:, :, :], res[0][:, :, :], ALU.add).then_inc(s_yb, 1)
                dve.wait_ge(s_yb, it + 1)
                for q in range(RG):
                    last = nc.vector.bn_stats(stats[:, q, :], ysum[:, q, :])
                last.then_inc(s_st, 1)
                dve.wait_ge(s_st, it + 1)
                nc.vector.tensor_copy(stat_in[:, :], stats[:, 0, 0:1])
                for q in range(RG):
                    last = nc.vector.bn_aggr(mv[:, q, :], stats[:, q, :])
                last.then_inc(s_mv, 1)

            def norm_apply(it):
                dve.wait_ge(s_rs, it + 1)
                for q in range(RG):
                    last = nc.vector.tensor_scalar(xn[:, q, :], ysum[:, q, :], mv[:, q, 0:1], rs[:, q:q + 1],
                                                   ALU.subtract, ALU.mult)
                last.then_inc(s_xn, 1)

            def stage_a(it, mlp):
                for c in range(CHUNKS):
                    transpose(it, c)
                    if not mlp and c == 0:
                        x_lo(0)
                    if c > 0:
                        lo(it, c - 1)
                    elif mlp:
                        lo(it - 1, CHUNKS - 1)
                    if not mlp and c % 2 and c < CHUNKS - 1:
                        x_lo((c + 1) // 2)
                    if mlp and c == 6:
                        norm_stats(it - 1)
                    if mlp and c == 7:
                        norm_apply(it - 1)

            stage_a(0, False)
            for k in range(2):
                dve.wait_ge(s_wTp, 4 * (k + 1))
                nc.vector.tensor_copy(w_T[:, 4 * k:4 * k + 4, :].rearrange("p a b -> p (a b)"), bank[5 + k][:, :])\
                    .then_inc(s_wT, 1)
            with dve.Fori(1, TILES) as it:
                stage_a(it, True)
            transpose(TILES, 0)
            lo(TILES - 1, CHUNKS - 1)
            transpose(TILES, 1)
            for h in range(H):
                dve.wait_ge(s_wcq, TAPS * (h + 1))
                nc.vector.tensor_copy(w_cv_sb[:, h, :, :].rearrange("p a b -> p (a b)"), bank[5 + h][:, :]).then_inc(s_wc, 1)
            transpose(TILES, 2)
            norm_stats(TILES - 1)
            norm_apply(TILES - 1)
            for c in range(3, CHUNKS):
                transpose(TILES, c)

            dve.wait_ge(s_xn, TILES)
            dve.sem_inc(s_aend, 1)
            dve.wait_ge(b_zero, 2)

            def front_g(a):
                dve.wait_ge(b_g, a + 1)
                for q in range(RG):
                    last = nc.vector.bn_stats(stats[:, q, :], g[:, q, :])
                last.then_inc(b_st, 1)
                dve.wait_ge(b_st, a + 1)
                nc.vector.tensor_copy(stat_in[:, :], stats[:, 0, 0:1])
                for q in range(RG):
                    last = nc.vector.bn_aggr(mv[:, q, :], stats[:, q, :])
                last.then_inc(b_mv, 1)

            def front_bclo(a, par):
                dve.wait_ge(b_bchi, a + 1)
                low = slice(4 * S, P)
                nc.vector.tensor_tensor(bc[par][low, :], M0[low, :], bc[par][low, :], ALU.subtract).then_inc(b_bc, 1)

            def front_spd(a, par):
                dve.wait_ge(b_spl, a + 1)
                nc.vector.scalar_tensor_tensor(sp_a[:, :, :], dtu[par][:, :, :], -1.0, sp_a[:, :, :], ALU.add, ALU.subtract)\
                    .then_inc(b_spd, 1)

            def tail_y(b, par):
                dve.wait_ge(b_y, (S - 1) * (b + 1))
                for h in range(H):
                    last = nc.vector.scalar_tensor_tensor(y[par][:, h, :], u[par][:, h, :], D_sb[:, h:h + 1], y[par][:, h, :],
                                                          ALU.mult, ALU.add)
                last.then_inc(b_yd, 1)

            def tail_stats(b, par):
                dve.wait_ge(b_out, b + 1)
                for q in range(RG):
                    last = nc.vector.bn_stats(stats2[:, q, :], O[:, q, :])
                last.then_inc(b_ost, 1)
                dve.wait_ge(b_ost, b + 1)
                nc.vector.tensor_copy(stat_in[:, :], stats2[:, 0, 0:1])
                for q in range(RG):
                    last = nc.vector.bn_aggr(mv2[:, q, :], stats2[:, q, :])
                last.then_inc(b_omv, 1)

            def window(b, par, tail, front):
                for n in range(S + 2):
                    if n < S and n not in POOL_B:
                        dve.wait_ge(b_B, S * b + n + 1)
                        if n == 0:
                            dve.wait_ge(b_dtu, b + 1)
                        wait(dve, b_scan, S * b + n - 1)
                        nc.vector.tensor_tensor(dBuV[v_slot(n, par)][:, :, 1:], dtu[par][:, :, :],
                                                BB[n % 2][:, :].unsqueeze(1).to_broadcast([P, H, TILE]), ALU.mult)\
                            .then_inc(b_dbuV, 1)
                    k = n - 1
                    if 0 <= k < S:
                        dve.wait_ge(b_dA, H * (S * b + k + 1))
                        if k in POOL_B:
                            dve.wait_ge(b_dbuP, NPB * b + nB(k) + 1)
                        else:
                            dve.wait_ge(b_dbuV, NVB * b + k - nB(k) + 1)
                        wait(dve, b_state, S * b + k - 1)
                        wait(dve, b_p, S * b + k - 1)
                        dve.wait_ge(b_start, S * b + k + 1)
                        flat = [a[:, :, :].rearrange("p h t -> p (h t)") for a in (hs[k % 2], dA[k % NDA], dBu(k, par))]
                        nc.vector.tensor_tensor_scan(flat[0], flat[1], flat[2], zero[:, :], ALU.mult, ALU.add)\
                            .then_inc(b_scan, 1)
                    k = n - 2
                    if k >= 0:
                        dve.wait_ge(b_C, S * b + k + 1)
                        dve.wait_ge(b_scan, S * b + k + 1)
                        wait(dve, b_y, (S - 1) * b + (max(k - NPR, 1) if k >= NPR else k - NPR + 1))
                        nc.vector.tensor_tensor(pr[k % NPR][:, :, :], hs[k % 2][:, :, 1:],
                                                CC[k % 2][:, :].unsqueeze(1).to_broadcast([P, H, TILE]), ALU.mult)\
                            .then_inc(b_p, 1)
                    if front:
                        if n == AT['dve_g']:
                            front_g(b + 1)
                        if n == AT['dve_bc']:
                            front_bclo(b + 1, 1 - par)
                        if n == AT['dve_sp']:
                            front_spd(b + 1, 1 - par)
                    if tail:
                        if n == AT['dve_y']:
                            tail_y(b - 1, 1 - par)
                        if n == AT['dve_tail']:
                            tail_stats(b - 1, 1 - par)

            dve.wait_ge(b_wdt, 1)
            nc.vector.tensor_tensor(w_dtl[:, :], w_dt_sb[:, :], w_dth[:, :], ALU.subtract).then_inc(b_wdt, 1)
            front_g(0)
            stage_a_over(dve)
            front_bclo(0, 0)
            front_spd(0, 0)
            dve.wait_ge(b_zero, 2 + NDA)
            window(0, 0, False, True)
            window(1, 1, True, True)
            with dve.Fori(0, 2) as i:
                window(2 * i + 2, 0, True, True)
                window(2 * i + 3, 1, True, True)
            window(6, 0, True, True)
            window(7, 1, True, False)
            tail_y(TILES - 1, 1)
            tail_stats(TILES - 1, 1)

        @block.tensor
        def _(pe):
            mm = nc.tensor.matmul
            def chunk(it, c):
                n = CHUNKS * it + c
                pe.wait_ge(s_al, n + 1)
                for k in range(2):
                    if c == 0:
                        wait(pe, s_h0[k], it)
                    if isinstance(it, int) and it == 0 and CH * c % XB == 0:
                        pe.wait_ge(s_xlo, 2 * (CH * c // XB) + k + 1)
                    for m in range(CH):
                        b = CH * c + m
                        cols = slice(m * TILE, (m + 1) * TILE)
                        for j, (w, v) in enumerate(((xh[k], ah), (xl[k], ah), (xh[k], al))):
                            last = mm(acc[k][:, :], w[:, b, :], v[c % 2][:, cols], start=(b == 0 and j == 0),
                                      stop=(b == KB - 1 and j == 2))
                    if c == CHUNKS - 1:
                        last.then_inc(s_acc[k], 1)
                        if k == 1:
                            pe.wait_ge(s_acc[1], it + 1)
                            pe.sem_inc(s_used, 1)
                    elif k == 1:
                        last.then_inc(s_used, 1)

            def layer(it, l):
                for k in range(2):
                    if l == 0:
                        pe.wait_ge(s_h0[k], it + 1)
                        pe.wait_ge(s_wT, 2)
                    else:
                        pe.wait_ge(s_hid, 2 * (LAYERS * it + l - 1) + k + 1)
                    mm(lay[k][:, :], w_T[:, LAYERS * k + l, :], hid[k][l][:, :], start=True, stop=True).then_inc(s_lay, 1)

            def merge(it):
                pe.wait_ge(s_hid, 2 * LAYERS * (it + 1))
                for q in range(RG):
                    for k in range(2):
                        last = mm(mrg[:, q, :], hid[k][LAYERS][:, P * q:P * q + P], w_T[:, 2 * LAYERS + k, :],
                                  start=(k == 0), stop=(k == 1))
                last.then_inc(s_mrg, 1)

            def weights():
                pe.wait_ge(s_w, 16 * WLOADS)
                pe.wait_ge(s_ident, 4)
                for j in range(2 * LAYERS + 2):
                    nc.tensor.transpose(bank[5 + j // 4][:, D * (j % 4):D * (j % 4) + D], w_nat[:, j, :], ident[:, :])\
                        .then_inc(s_wTp, 1)
                for h in range(H):
                    nc.tensor.transpose(bank[7][:, P * h:P * h + P], w_in_sb[:, P * h:P * h + P], ident[:, :]).then_inc(s_wcp, 1)

            def stage_a(it, mlp):
                for c in range(CHUNKS):
                    chunk(it, c)
                    if mlp and c < LAYERS:
                        layer(it - 1, c)
                    if mlp and c == LAYERS:
                        merge(it - 1)
                    if not mlp and c == CHUNKS - 3:
                        weights()

            stage_a(0, False)
            with pe.Fori(1, TILES) as it:
                stage_a(it, True)
            pe.wait_ge(s_wcs, H * TAPS)
            pe.wait_ge(s_wT, 2)
            for h in range(H):
                for k in range(TAPS):
                    nc.tensor.transpose(bank[5 + h][:, P * k:P * k + P], w_nat[:, TAPS * h + k, :], ident[:, :])\
                        .then_inc(s_wcq, 1)
            def adj_tile0(blocks):
                for b in blocks:
                    c, m = b // CH, b % CH
                    if m == 0:
                        pe.wait_ge(s_at, CHUNKS * TILES + c + 1)
                        pe.wait_ge(b_xm, 16 * (c + 1))
                    last = mm(accB[:, :], xm[:, b, :], at[c % 2][:, m, :], start=(b == 0), stop=(b == KB - 1))
                    if b == KB - 1:
                        last.then_inc(b_acc, 1)
                    elif m == CH - 1:
                        last.then_inc(s_used, 1)

            adj_tile0(range(1))
            for l in range(LAYERS):
                layer(TILES - 1, l)
                adj_tile0(range(l + 1, l + 2))
            merge(TILES - 1)
            adj_tile0(range(LAYERS + 1, KB))


            def adj_blocks(a, b0, b1):
                for b in range(b0, b1):
                    c, m = b // CH, b % CH
                    if m == 0:
                        pe.wait_ge(b_adj[c % NADJ], 16 * (CHUNKS // NADJ * (a - 1) + c // NADJ + 1))
                    if b == 0:
                        wait(pe, b_ax, a)
                    last = mm(accB[:, :], xm[:, b, :], adjc[c % NADJ][:, m, :], start=(b == 0), stop=(b == KB - 1))
                    if b == KB - 1:
                        last.then_inc(b_acc, 1)
                        pe.wait_ge(b_acc, a + 1)
                        pe.sem_inc(b_adjused, 1)
                    elif m == CH - 1:
                        last.then_inc(b_adjused, 1)

            def front_gcn(a):
                pe.wait_ge(b_ax, a + 1)
                wait(pe, b_spab, 4 * a)
                for q in range(RG):
                    mm(M0g[:, q, :], axT[:, P * q:P * q + P], gcn_w_sb[:, :], start=True, stop=False)
                    last = mm(M0g[:, q, :], ones[0:1, :], gcn_b_sb[0:1, :], start=False, stop=True)
                last.then_inc(b_gcn, 1)

            def front_tr(a):
                pe.wait_ge(b_hn, RG * (a + 1))
                for q in range(RG):
                    last = nc.tensor.transpose(M1[:, P * q:P * q + P], hn[:, q, :], ident[:, :])
                last.then_inc(b_tr, 1)

            def front_xc(a, j0, j1):
                for j in range(j0, j1):
                    h, k = j // TAPS, j % TAPS
                    if j == 0:
                        pe.wait_ge(b_hT, a + 1)
                        pe.wait_ge(b_g, a + 1)
                    last = mm((M0, M1)[h][:, :], w_cv_sb[:, h, k, :], hT[:, k:k + TILE], start=(k == 0), stop=(k == TAPS - 1))
                    if k == TAPS - 1:
                        last.then_inc(b_xc, 1)

            def front_z(a, h):
                m = (M0, M1)[h]
                pe.wait_ge(b_u, H * a + h + 1)
                mm(m[:, :], w_in_sb[:, DI + P * h:DI + P * h + P], hT[:, TAPS - 1:], start=True, stop=True).then_inc(b_z, 1)

            def front_dbc(a, par):
                pe.wait_ge(b_sz, 2 * a + 2)
                pe.wait_ge(b_u, H * (a + 1))
                for h in range(H):
                    last = mm(M0[:, :], w_xp_sb[:, h, :], u[par][:, h, :], start=(h == 0), stop=(h == 1))
                last.then_inc(b_dbc, 1)

            def front_dtp(a, par):
                pe.wait_ge(b_bc, a + 1)
                for h, m in enumerate((M1, M0)):
                    mm(m[:, :], w_dth[:, P * h:P * h + P], bc[par][:, :], start=True, stop=False)
                    mm(m[:, :], w_dtl[:, P * h:P * h + P], bc[par][:, :], start=False, stop=True).then_inc(b_dtp, 1)

            def spread_B(b, n, par):
                if n == 0:
                    pe.wait_ge(b_bc, b + 1)
                k, bb = (n - 2, b) if n >= 2 else (n - 2 + S, b - 1)
                if not (isinstance(bb, int) and bb < 0):
                    if k in POOL_B:
                        pe.wait_ge(b_Bsb, NPB * bb + nB(k) + 1)
                    else:
                        pe.wait_ge(b_dbuV, NVB * bb + k - nB(k) + 1)
                mm(BB[n % 2][:, :], sel[:, n, :], bc[par][:, :], start=True, stop=True).then_inc(b_B, 1)

            def spread_C(b, n, par):
                wait(pe, b_p, S * b + n - 1)
                mm(CC[n % 2][:, :], sel[:, S + n, :], bc[par][:, :], start=True, stop=True).then_inc(b_C, 1)

            def tail_out(b, par):
                pe.wait_ge(b_yg, b + 1)
                wait(pe, b_on, RG * b)
                pe.wait_ge(b_res[par], 8 * (b - par) + 16)
                for q in range(RG):
                    mm(O[:, q, :], ident[:, :], res[par][:, q, :], start=True, stop=False)
                    for h in range(H):
                        last = mm(O[:, q, :], y[par][:, h, P * q:P * q + P], w_out_sb[:, h, :], start=False, stop=(h == 1))
                last.then_inc(b_out, 1)


            def window(b, par, tail, front, adj_):
                spread_B(b, 0, par)
                for n in range(S):
                    if n + 1 < S:
                        spread_B(b, n + 1, par)
                    if AT['pe_C'] == 0:
                        spread_C(b, n, par)
                    if front:
                        if n == 0:
                            front_gcn(b + 1)
                        if n == AT['pe_tr']:
                            front_tr(b + 1)
                        front_xc(b + 1, sum(CONV[:n]), sum(CONV[:n + 1]))
                        if n == AT['pe_z']:
                            front_z(b + 1, 0)
                            front_z(b + 1, 1)
                        if n == AT['pe_dbc']:
                            front_dbc(b + 1, 1 - par)
                        if n == AT['pe_dt']:
                            front_dtp(b + 1, 1 - par)
                    if tail and n == AT['pe_out']:
                        tail_out(b - 1, 1 - par)
                    if adj_:
                        adj_blocks(b + 2, sum(PLAN[:n]), sum(PLAN[:n + 1]))
                    if AT['pe_C'] == 1:
                        spread_C(b, n, par)

            pe.wait_ge(s_wc, H)
            pe.wait_ge(b_wdt, 2)
            done = 0
            pieces = (lambda: front_gcn(0), lambda: front_tr(0), lambda: front_xc(0, 0, TAPS), lambda: front_xc(0, TAPS, H * TAPS),
                      lambda: (front_z(0, 0), front_z(0, 1)), lambda: front_dbc(0, 0), lambda: front_dtp(0, 0), lambda: None)
            for blocks, piece in zip(FILL, pieces):
                adj_blocks(1, done, done + blocks)
                done += blocks
                piece()
            pe.wait_ge(b_sel, 4)
            window(0, 0, False, True, True)
            window(1, 1, True, True, True)
            with pe.Fori(0, 2) as i:
                window(2 * i + 2, 0, True, True, True)
                window(2 * i + 3, 1, True, True, True)
            window(6, 0, True, True, False)
            window(7, 1, True, False, False)
            tail_out(TILES - 1, 1)


_INS = ['x', 'adj', 'L0_gnn_x2', 'L0_gnn_eps1', 'L0_gnn_eps2', 'L0_gnn_W1', 'L0_gnn_b1', 'L0_gnn_W2', 'L0_gnn_b2',
        'L0_gnn_Wm', 'L0_gnn_bm', 'L1_gnn_gcn_w', 'L1_gnn_gcn_b', 'L1_gnn_ln_g', 'L1_gnn_ln_b', 'L1_gnn_w_in',
        'L1_gnn_conv_w', 'L1_gnn_conv_b', 'L1_gnn_w_xp', 'L1_gnn_w_dt', 'L1_gnn_b_dt', 'L1_gnn_A_log',
        'L1_gnn_D_skip', 'L1_gnn_w_out']


def kernel(**inputs):
    import numpy as np
    import concourse.bacc as bacc
    from concourse import mybir as _mybir
    from concourse.bass_utils import run_bass_kernel_spmd

    nc = bacc.Bacc("TRN2", target_bir_lowering=False, num_devices=1)
    arrays, args = {}, []
    for name in _INS:
        a = np.ascontiguousarray(inputs[name])
        arrays[f"in_{name}"] = a
        args.append(nc.dram_tensor(f"in_{name}", a.shape, _mybir.dt.from_np(a.dtype), kind="ExternalInput").ap())
    out = nc.dram_tensor("out", (4096, 128), _mybir.dt.float32, kind="ExternalOutput").ap()
    gnn_mamba(nc, *args, out)
    r = run_bass_kernel_spmd(nc, [arrays], core_ids=[0])
    return r.results[0]["out"]
```

```python
from contextlib import ExitStack

import concourse.bass as bass
from concourse import mybir

F32 = mybir.dt.float32
F32R = mybir.dt.float32r
ALU = mybir.AluOpType
ACT = mybir.ActivationFunctionType

P = 128
N = 4096
D = 128
TILE = 512
TILES = N // TILE
KB = N // P
CH = 4
CHUNKS = KB // CH
CHC = CH * TILE
Q = 4
GROUPS = TILE // 32
RG = TILE // P
LAYERS = 3
DI = 256
H = 2
S = 16
R = 8
TAPS = 4
EPS = 1e-5


def wait(eng, sem, value):
    if not isinstance(value, int) or value > 0:
        eng.wait_ge(sem, value)


AT = dict(pool_rs=2, pool_gate=3, pool_tail_rs=7, pool_dt=11, act_hn=5, act_hT=6, act_silu=9, act_bc=10,
          act_sp=11, act_exp=13, act_tail=10, dve_g=1, dve_bc=9, dve_sp=12, dve_y=4, dve_tail=6, pe_tr=3,
          pe_z=6, pe_dbc=7, pe_dt=9, pe_out=4, act_B=1, act_g=1, act_start=1, pool_ahead=0)
FILL = (3, 4, 3, 0, 0, 0, 3, 10, 9)
CONV = (0, 0, 0, 0, 2, 1, 5, 0, 0, 0, 0, 0, 0, 0, 0, 0)
PLAN = (3, 2, 3, 2, 0, 1, 1, 0, 0, 3, 3, 5, 1, 3, 3, 2)
POOL = (3, 7, 10)


def gnn_mamba(nc, x, adj, x2, eps1, eps2, W1, b1, W2, b2, Wm, bm, gcn_w, gcn_b, ln_g, ln_b, w_in, conv_w,
              conv_b, w_xp, w_dt, b_dt, A_log, D_skip, w_out, out):
    POOL_B = POOL
    ctx = ExitStack()
    with ctx:
        def sem(name):
            return ctx.enter_context(nc.semaphore(name))

        def sb(name, shape, dt=F32, stack=ctx):
            return stack.enter_context(nc.sbuf_tensor(name, shape, dt))

        adjT = nc.dram_tensor("adjT", ((TILES - 1) * CHUNKS * P, CHC), F32, kind="Internal").ap()
        mid = nc.dram_tensor("mid", (N, D), F32, kind="Internal").ap()

        ident = sb("ident", [P, P])
        neg_half = sb("neg_half", [P, RG])
        eps_ln = sb("eps_ln", [P, RG])
        zero = sb("zero", [P, 1])
        ones = sb("ones", [P, P])
        neg_one = sb("neg_one", [P, RG])
        gcn_w_sb = sb("gcn_w_sb", [P, D])
        gcn_b_sb = sb("gcn_b_sb", [P, D])
        bm_sb = sb("bm_sb", [P, D])
        ln_g_sb = sb("ln_g_sb", [P, 1])
        ln_b_sb = sb("ln_b_sb", [P, 1])
        w_in_sb = sb("w_in_sb", [P, 2 * DI])
        conv_w_sb = sb("conv_w_sb", [P, H, TAPS])
        conv_b_sb = sb("conv_b_sb", [P, H])
        w_xp_sb = sb("w_xp_sb", [P, H, P])
        w_dt_sb = sb("w_dt_sb", [P, DI])
        w_cv_sb = sb("w_cv_sb", [P, H, TAPS, P])
        b_dt_sb = sb("b_dt_sb", [P, H])
        A_sb = sb("A_sb", [P, H, S])
        D_sb = sb("D_sb", [P, H])
        w_out_sb = sb("w_out_sb", [P, H, D])
        eps_sb = sb("eps_sb", [P, 2])
        bias_sb = sb("bias_sb", [P, 2, LAYERS])
        stats = sb("stats", [P, RG, 6])
        stat_in = sb("stat_in", [P, 1])
        mv = sb("mv", [P, RG, 2])
        ve = sb("ve", [P, RG])
        rs = sb("rs", [P, RG])
        mr = sb("mr", [P, RG])
        nb = sb("nb", [P, RG])
        stats2 = sb("stats2", [P, RG, 6])
        mv2 = sb("mv2", [P, RG, 2])
        ve2 = sb("ve2", [P, RG])
        rs2 = sb("rs2", [P, RG])
        mr2 = sb("mr2", [P, RG])
        nb2 = sb("nb2", [P, RG])
        res = [sb(f"res{i}", [P, RG, D]) for i in range(2)]
        state = sb("state", [P, S, H])
        xm = sb("xm", [P, KB, D])

        A = ExitStack()
        xh = [sb(f"xh{k}", [P, KB, D], F32R, A) for k in range(2)]
        xl = [sb(f"xl{k}", [P, KB, D], F32R, A) for k in range(2)]
        ah = [sb(f"ah{k}", [P, CHC], F32R, A) for k in range(2)]
        al = [sb(f"al{k}", [P, CHC], F32R, A) for k in range(2)]
        NROWS = 4
        rows = [sb(f"rows{k}", [P, GROUPS, P], F32, A) for k in range(NROWS)]
        at = [sb(f"at{k}", [P, CH, TILE], F32, A) for k in range(2)]
        w_nat = sb("w_nat", [P, 2 * LAYERS + 2, D], F32, A)
        w_T = sb("w_T", [P, 2 * LAYERS + 2, D], F32, A)
        A1 = ExitStack()
        xs = [xm, sb("xs1", [P, KB, D], F32, A1)]
        A1.close()
        hid = [[sb(f"hid{k}_{l}", [P, TILE], F32, A) for l in range(LAYERS + 1)] for k in range(2)]
        ysum = sb("ysum", [P, RG, D], F32, A)
        xn = sb("xn", [P, RG, D], F32, A)
        A.close()

        B = ExitStack()
        NADJ = 4
        adjc = [sb(f"adjc{k}", [P, CH, TILE], F32, B) for k in range(NADJ)]
        sel = sb("sel", [P, 2 * S], F32R, B)
        w_dth = sb("w_dth", [P, DI], F32R, B)
        w_dtl = sb("w_dtl", [P, DI], F32R, B)
        axT = sb("axT", [P, TILE], F32, B)
        g = sb("g", [P, RG, D], F32, B)
        hn = sb("hn", [P, RG, D], F32, B)
        hT = sb("hT", [P, TAPS - 1 + TILE], F32, B)
        u = [sb(f"u{k}", [P, H, TILE], F32, B) for k in range(2)]
        sz = [sb(f"sz{k}", [P, H, TILE], F32, B) for k in range(2)]
        sp_a = sb("sp_a", [P, H, TILE], F32, B)
        sp_r = sb("sp_r", [P, H, TILE], F32, B)
        dt_ = [sb(f"dt{k}", [P, H, TILE], F32, B) for k in range(2)]
        dtu = [sb(f"dtu{k}", [P, H, TILE], F32, B) for k in range(2)]
        bc = [sb(f"bc{k}", [P, TILE], F32R, B) for k in range(2)]
        NDA, NPR, NHS = 4, 4, 4
        LAG = 4
        dA = [sb(f"dA{k}", [P, H, 1 + TILE], F32, B) for k in range(NDA)]
        dBuV = [sb(f"dBuV{k}", [P, H, 1 + TILE], F32, B) for k in range(2)]
        dBuP = [sb(f"dBuP{k}", [P, H, 1 + TILE], F32, B) for k in range(2)]
        hs = [sb(f"hs{k}", [P, H, 1 + TILE], F32, B) for k in range(NHS)]
        pr = [sb(f"pr{k}", [P, H, TILE], F32, B) for k in range(NPR)]
        y = [sb(f"y{k}", [P, H, TILE], F32, B) for k in range(2)]
        b_sb = [sb(f"b_sb{k}", [P, TILE], F32, B) for k in range(2)]
        o_n = sb("o_n", [P, RG, D], F32, B)
        B.close()

        bank = [ctx.enter_context(nc.psum_tensor(f"bank{i}", [P, TILE], F32)) for i in range(8)]
        acc = [bank[0], bank[1]]
        lay = [bank[2], bank[3]]
        mrg = bank[4][:, :].rearrange("p (g d) -> p g d", g=RG)
        accB, M0, M1 = bank[7], bank[1], bank[2]
        BB = [bank[3], bank[5]]
        CC = [bank[4], bank[6]]
        O = bank[0][:, :].rearrange("p (g d) -> p g d", g=RG)
        M0g = M0[:, :].rearrange("p (g d) -> p g d", g=RG)

        weights_in = sem("weights_in")
        consts_set = sem("consts_set")
        XP = 4
        x_in = [sem(f"x_in{k}") for k in range(2 * XP)]
        x_high, x_low = sem("x_high"), sem("x_low")
        weights_turned, weights_T_ready = sem("weights_turned"), sem("weights_T_ready")
        rows_in = [sem(f"rows_in{k}") for k in range(NROWS)]
        chunk_turned = sem("chunk_turned")
        chunk_stored = [sem(f"chunk_stored{k}") for k in range(2)]
        chunk_high, chunk_low = sem("chunk_high"), sem("chunk_low")
        chunk_multiplied = sem("chunk_multiplied")
        ax_summed = [sem(f"ax_summed{k}") for k in range(2)]
        layer_in = [sem(f"layer_in{k}") for k in range(2)]
        layer_product, layer_out = sem("layer_product"), sem("layer_out")
        stacks_merged = sem("stacks_merged")
        bm_added, x_added = sem("bm_added"), sem("x_added")
        a_stats, a_mean_var = sem("a_stats"), sem("a_mean_var")
        a_var_eps, a_inv_dev = sem("a_var_eps"), sem("a_inv_dev")
        x1_normed, x1_stored, x_tile_in = sem("x1_normed"), sem("x1_stored"), sem("x_tile_in")
        small_prep = sem("small_prep")
        w_in_turned, w_in_tapped = sem("w_in_turned"), sem("w_in_tapped")
        w_taps_turned, w_taps_ready = sem("w_taps_turned"), sem("w_taps_ready")
        engines_through = sem("engines_through")

        x1_in = sem("x1_in")
        x1_tile_in = [sem(f"x1_tile_in{k}") for k in range(2)]
        adjT_in = [sem(f"adjT_in{k}") for k in range(NADJ)]
        adjT_multiplied = sem("adjT_multiplied")
        ax1_summed, ax1_ready = sem("ax1_summed"), sem("ax1_ready")
        gcn_product, gcn_relu = sem("gcn_product"), sem("gcn_relu")
        f_stats, f_mean_var, f_var_eps, f_inv_dev = sem("f_stats"), sem("f_mean_var"), sem("f_var_eps"), sem("f_inv_dev")
        f_mean_scaled, f_mean_negated, f_normed = sem("f_mean_scaled"), sem("f_mean_negated"), sem("f_normed")
        h_turned, history_kept, h_ready = sem("h_turned"), sem("history_kept"), sem("h_ready")
        conv_summed, z_product = sem("conv_summed"), sem("z_product")
        u_ready, gate_ready = sem("u_ready"), sem("gate_ready")
        bcdt_product, bcdt_high, bcdt_low = sem("bcdt_product"), sem("bcdt_high"), sem("bcdt_low")
        dt_product = sem("dt_product")
        sp_abs_relu = sem("sp_abs_relu")
        sp_exp, sp_one_plus, sp_log = sem("sp_exp"), sem("sp_one_plus"), sem("sp_log")
        sp_error, sp_corrected, dt_ready = sem("sp_error"), sem("sp_corrected"), sem("dt_ready")
        dtu_ready = sem("dtu_ready")
        B_spread, C_spread, B_copied = sem("B_spread"), sem("C_spread"), sem("B_copied")
        dA_ready, start_set = sem("dA_ready"), sem("start_set")
        dBu_by_dve, dBu_by_pool = sem("dBu_by_dve"), sem("dBu_by_pool")
        scanned, state_kept = sem("scanned"), sem("state_kept")
        C_multiplied, y_added = sem("C_multiplied"), sem("y_added")
        y_skipped, y_gated, projected = sem("y_skipped"), sem("y_gated"), sem("projected")
        o_stats, o_mean_var, o_var_eps, o_inv_dev = sem("o_stats"), sem("o_mean_var"), sem("o_var_eps"), sem("o_inv_dev")
        o_mean_scaled, o_mean_negated, o_normed = sem("o_mean_scaled"), sem("o_mean_negated"), sem("o_normed")
        out_stored = sem("out_stored")
        zeroed, selectors_ready, w_dt_parts = sem("zeroed"), sem("selectors_ready"), sem("w_dt_parts")

        WLOADS = 32
        XB = KB // XP

        def nB(n):
            return sum(1 for k in POOL_B if k < n)

        NPB = len(POOL_B)
        NVB = S - NPB

        def dve_slot(n, par):
            return (n - nB(n) + NVB * par) % 2

        def pool_slot(n, par):
            return (nB(n) + NPB * par) % 2

        def dBu(n, par):
            return dBuP[pool_slot(n, par)] if n in POOL_B else dBuV[dve_slot(n, par)]

        def stage_a_over(eng):
            eng.wait_ge(engines_through, 3)
            eng.wait_ge(ax1_summed, 1)

        block = ctx.enter_context(nc.Block())

        def load_rows(eng, quads, it, c):
            for q in quads:
                src = adj[bass.ds(it * TILE, TILE), TILE * c + P * q:TILE * c + P * q + P].rearrange("(g i) c -> i g c", g=GROUPS)
                eng.dma_start(rows[c % NROWS][32 * q:32 * q + 32, :, :], src).then_inc(rows_in[c % NROWS], 16)

        @block.sync
        def _(sp):
            def load_x(part):
                tiles = slice(XB // CH * part, XB // CH * (part + 1))
                for k, src in enumerate((x, x2)):
                    sp.dma_start(xs[k][:, XB * part:XB * (part + 1), :].rearrange("p (t m) d -> p t (m d)", m=CH),
                                 src.rearrange("(t p m) d -> p t (m d)", p=P, m=CH)[:, tiles])\
                        .then_inc(x_in[2 * part + k], 16)

            load_rows(sp, (0, 1), 0, 0)
            load_x(0)
            for c in range(1, NROWS):
                load_rows(sp, (0, 1), 0, c)
                load_x(c)

            def stage_a(it, store):
                for c in range(CHUNKS):
                    sp.wait_ge(chunk_turned, CHUNKS * it + c + 1)
                    if store:
                        sp.dma_start(adjT[bass.ds(((it - 1) * CHUNKS + c) * P, P), :],
                                     at[c % 2][:, :, :].rearrange("p m t -> p (m t)")).then_inc(chunk_stored[c % 2], 16)
                    after = it + (c + NROWS) // CHUNKS
                    load_rows(sp, (0, 1), 0 if isinstance(after, int) and after == TILES else after, (c + NROWS) % CHUNKS)

            stage_a(0, False)
            for k in range(2):
                sp.sem_inc(chunk_stored[k], 16)
            with sp.Fori(1, TILES - 1) as it:
                stage_a(it, True)
            stage_a(TILES - 1, True)
            for k in range(2):
                sp.wait_ge(chunk_stored[k], 16 * ((TILES - 1) * CHUNKS // 2 + 1))
            sp.sem_inc(engines_through, 1)
            sp.wait_ge(chunk_multiplied, TILES * CHUNKS)
            for c in range(NROWS, CHUNKS):
                sp.wait_ge(chunk_turned, CHUNKS * TILES + c - NROWS + 1)
                load_rows(sp, range(Q), 0, c)

            def load_adj(a, chunks):
                for c in chunks:
                    wait(sp, adjT_multiplied, CHUNKS * (a - 1) + c - NADJ + 1)
                    sp.dma_start(adjc[c % NADJ][:, :, :].rearrange("p m t -> p (m t)"),
                                 adjT[bass.ds(((a - 1) * CHUNKS + c) * P, P), :]).then_inc(adjT_in[c % NADJ], 16)

            def load_res(b, par):
                wait(sp, projected, b - 1)
                sp.dma_start(res[par][:, :, :], mid[bass.ds(b * TILE, TILE), :].rearrange("(g p) d -> p g d", g=RG))\
                    .then_inc(x1_tile_in[par], 16)

            def store(b):
                sp.wait_ge(o_normed, RG * (b + 1))
                sp.dma_start(out[bass.ds(b * TILE, TILE), :].rearrange("(g p) d -> p g d", g=RG), o_n[:, :, :])\
                    .then_inc(out_stored, 16)

            def window(b, par, tail, adj_):
                load_res(b, par)
                if adj_:
                    load_adj(b + 2, range(0, CHUNKS - 2))
                if tail:
                    store(b - 1)
                if adj_:
                    load_adj(b + 2, range(CHUNKS - 2, CHUNKS))

            load_adj(1, range(CHUNKS))
            window(0, 0, False, True)
            window(1, 1, True, True)
            with sp.Fori(0, 2) as i:
                window(2 * i + 2, 0, True, True)
                window(2 * i + 3, 1, True, True)
            window(6, 0, True, False)
            window(7, 1, True, False)
            store(TILES - 1)
            sp.wait_ge(out_stored, 16 * TILES)

        @block.gpsimd
        def _(pool):
            nc.gpsimd.memset(w_xp_sb[:, :, :], 0.0).then_inc(consts_set, 1)
            nc.gpsimd.memset(w_dt_sb[:, :], 0.0).then_inc(consts_set, 1)
            pool.wait_ge(consts_set, 2)
            loads = []

            def load(dst, src):
                loads.append(dst)
                pool.dma_start(dst, src).then_inc(weights_in, 16)

            for k in range(2):
                pool.wait_ge(x_in[k], 16)
            load(w_nat[:, 0:LAYERS, :], W1.rearrange("l o d -> o l d"))
            load(w_nat[:, LAYERS:2 * LAYERS, :], W2.rearrange("l o d -> o l d"))
            load(w_nat[:, 2 * LAYERS:, :].rearrange("p k d -> p (k d)"), Wm)
            for k, b in enumerate((b1, b2)):
                for l in range(LAYERS):
                    load(bias_sb[:, k, l:l + 1], b[l].rearrange("(p o) -> p o", o=1))
            load(eps_sb[:, 0:1], eps1.partition_broadcast(P))
            load(eps_sb[:, 1:2], eps2.partition_broadcast(P))
            load(bm_sb[:, :], bm.partition_broadcast(P))
            load(gcn_b_sb[:, :], gcn_b.partition_broadcast(P))
            load(gcn_w_sb[:, :], gcn_w)
            load(ln_g_sb[:, :], ln_g.rearrange("(p o) -> p o", o=1))
            load(ln_b_sb[:, :], ln_b.rearrange("(p o) -> p o", o=1))
            load(w_in_sb[:, :], w_in)
            load(conv_w_sb[:, :, :], conv_w.rearrange("(h p) k -> p h k", h=H))
            for at_ in (2 * S, 6 * S):
                load(w_dt_sb[at_:at_ + R, :], w_dt)
            load(A_sb[:, :, :], A_log.rearrange("(h p) s -> p h s", h=H))
            load(w_out_sb[:, :, :], w_out.rearrange("(h p) d -> p h d", h=H))
            for h in range(H):
                for dst, src in ((conv_b_sb, conv_b), (b_dt_sb, b_dt), (D_sb, D_skip)):
                    load(dst[:, h:h + 1], src.rearrange("(h p o) -> h p o", h=H, o=1)[h])
            v = w_xp.rearrange("(h p) j -> p h j", h=H)
            for half in range(2):
                load(w_xp_sb[:, :, 4 * S * half:4 * S * half + 2 * S], v[:, :, R:])
                load(w_xp_sb[:, :, 4 * S * half + 2 * S:4 * S * half + 2 * S + R], v[:, :, 0:R])
            assert len(loads) == WLOADS, len(loads)

            nc.gpsimd.memset(ident[:, :], 0.0).then_inc(consts_set, 1)
            pool.wait_ge(consts_set, 3)
            nc.gpsimd.affine_select(out=ident[:, :], in_=ident[:, :], compare_op=ALU.not_equal, fill=1.0, base=0,
                                    pattern=[[-1, P]], channel_multiplier=1).then_inc(consts_set, 1)
            nc.gpsimd.memset(neg_half[:, :], -0.5).then_inc(consts_set, 1)
            nc.gpsimd.memset(eps_ln[:, :], EPS).then_inc(consts_set, 1)
            nc.gpsimd.memset(neg_one[:, :], -1.0).then_inc(consts_set, 1)
            nc.gpsimd.memset(zero[:, :], 0.0).then_inc(consts_set, 1)
            nc.gpsimd.memset(ones[:, :], 1.0).then_inc(consts_set, 1)
            pool.wait_ge(consts_set, 9)

            def load_res(it, par):
                pool.dma_start(res[par][:, :, :], x[bass.ds(it * TILE, TILE), :].rearrange("(g p) d -> p g d", g=RG))\
                    .then_inc(x_tile_in, 16)

            def norm(it):
                pool.wait_ge(a_mean_var, it + 1)
                nc.gpsimd.tensor_tensor(ve[:, :], mv[:, :, 1], eps_ln[:, :], ALU.add).then_inc(a_var_eps, 1)
                pool.wait_ge(a_var_eps, it + 1)
                nc.gpsimd.tensor_tensor(rs[:, :], ve[:, :], neg_half[:, :], ALU.pow).then_inc(a_inv_dev, 1)
                pool.wait_ge(x1_normed, it + 1)
                pool.dma_start(mid[bass.ds(it * TILE, TILE), :].rearrange("(g p) d -> p g d", g=RG), xn[:, :, :])\
                    .then_inc(x1_stored, 16)
                pool.wait_ge(x1_stored, 16 * it + 16)
                pool.dma_start(xm[:, bass.ds(it * CH, CH), :].rearrange("p m d -> p (m d)"),
                               mid[bass.ds(it * TILE, TILE), :].rearrange("(p m) d -> p (m d)", m=CH)).then_inc(x1_in, 16)

            load_res(0, 0)
            with pool.Fori(0, TILES - 1) as it:
                norm(it)
                load_res(it + 1, 0)
            pool.wait_ge(chunk_multiplied, TILES * CHUNKS)
            nc.gpsimd.memset(state[:, :, :], 0.0).then_inc(zeroed, 1)
            nc.gpsimd.memset(hT[:, :], 0.0).then_inc(zeroed, 1)
            norm(TILES - 1)
            pool.wait_ge(x1_in, 16 * TILES)
            pool.sem_inc(engines_through, 1)


            def front_rs(a):
                pool.wait_ge(f_mean_var, a + 1)
                nc.gpsimd.tensor_tensor(ve[:, :], mv[:, :, 1], eps_ln[:, :], ALU.add).then_inc(f_var_eps, 1)
                pool.wait_ge(f_var_eps, a + 1)
                nc.gpsimd.tensor_tensor(rs[:, :], ve[:, :], neg_half[:, :], ALU.pow).then_inc(f_inv_dev, 1)
                pool.wait_ge(f_inv_dev, a + 1)
                nc.gpsimd.tensor_tensor(mr[:, :], mv[:, :, 0], rs[:, :], ALU.mult).then_inc(f_mean_scaled, 1)
                pool.wait_ge(f_mean_scaled, a + 1)
                nc.gpsimd.tensor_tensor(nb[:, :], mr[:, :], neg_one[:, :], ALU.mult).then_inc(f_mean_negated, 1)

            def front_dt(a, par, step):
                if step == 0:
                    pool.wait_ge(sp_error, a + 1)
                    nc.gpsimd.tensor_tensor(dt_[par][:, :, :], dt_[par][:, :, :], sp_a[:, :, :], ALU.subtract)\
                        .then_inc(sp_corrected, 1)
                elif step == 1:
                    pool.wait_ge(sp_corrected, a + 1)
                    nc.gpsimd.tensor_tensor(dt_[par][:, :, :], dt_[par][:, :, :], sp_r[:, :, :], ALU.add).then_inc(dt_ready, 1)
                else:
                    pool.wait_ge(dt_ready, a + 1)
                    nc.gpsimd.tensor_tensor(dtu[par][:, :, :], dt_[par][:, :, :], u[par][:, :, :], ALU.mult)\
                        .then_inc(dtu_ready, 1)

            def tail_gate(b, par):
                pool.wait_ge(y_skipped, b + 1)
                nc.gpsimd.tensor_tensor(y[par][:, :, :], y[par][:, :, :], sz[par][:, :, :], ALU.mult).then_inc(y_gated, 1)

            def tail_rs(b):
                pool.wait_ge(o_mean_var, b + 1)
                nc.gpsimd.tensor_tensor(ve2[:, :], mv2[:, :, 1], eps_ln[:, :], ALU.add).then_inc(o_var_eps, 1)
                pool.wait_ge(o_var_eps, b + 1)
                nc.gpsimd.tensor_tensor(rs2[:, :], ve2[:, :], neg_half[:, :], ALU.pow).then_inc(o_inv_dev, 1)
                pool.wait_ge(o_inv_dev, b + 1)
                nc.gpsimd.tensor_tensor(mr2[:, :], mv2[:, :, 0], rs2[:, :], ALU.mult).then_inc(o_mean_scaled, 1)
                pool.wait_ge(o_mean_scaled, b + 1)
                nc.gpsimd.tensor_tensor(nb2[:, :], mr2[:, :], neg_one[:, :], ALU.mult).then_inc(o_mean_negated, 1)

            def window(b, par, tail, front):
                for step in range(S + 2):
                    n = step + AT['pool_ahead']
                    if n in POOL_B:
                        pool.wait_ge(B_copied, NPB * b + nB(n) + 1)
                        before = [j for j in range(-S, n) if j % S in POOL_B][-2]
                        wait(pool, scanned, S * b + before + 1)
                        pool.wait_ge(dtu_ready, b + 1)
                        nc.gpsimd.tensor_tensor(dBu(n, par)[:, :, 1:], dtu[par][:, :, :],
                                                b_sb[pool_slot(n, par)][:, :].unsqueeze(1).to_broadcast([P, H, TILE]),
                                                ALU.mult).then_inc(dBu_by_pool, 1)
                    n = step
                    k = n - 2
                    if k == 1:
                        wait(pool, projected, b - 1)
                        pool.wait_ge(C_multiplied, S * b + 2)
                        nc.gpsimd.tensor_tensor(y[par][:, :, :], pr[0][:, :, :], pr[1][:, :, :], ALU.add).then_inc(y_added, 1)
                    elif k > 1:
                        pool.wait_ge(C_multiplied, S * b + k + 1)
                        pool.wait_ge(y_added, (S - 1) * b + k - 1)
                        nc.gpsimd.tensor_tensor(y[par][:, :, :], y[par][:, :, :], pr[k % NPR][:, :, :], ALU.add).then_inc(y_added, 1)
                    if front and n == AT['pool_rs']:
                        front_rs(b + 1)
                    if tail and n == AT['pool_gate']:
                        tail_gate(b - 1, 1 - par)
                    if tail and n == AT['pool_tail_rs']:
                        tail_rs(b - 1)
                    if front and 0 <= n - AT['pool_dt'] < 3:
                        front_dt(b + 1, 1 - par, n - AT['pool_dt'])

            front_rs(0)
            stage_a_over(pool)
            for a in dA:
                nc.gpsimd.memset(a[:, :, 0:1], 0.0).then_inc(zeroed, 1)
            window(0, 0, False, True)
            window(1, 1, True, True)
            with pool.Fori(0, 2) as i:
                window(2 * i + 2, 0, True, True)
                window(2 * i + 3, 1, True, True)
            window(6, 0, True, True)
            window(7, 1, True, False)
            tail_rs(TILES - 1)

        @block.scalar
        def _(act):
            for c in range(NROWS):
                load_rows(act, (2, 3), 0, c)
            act.preload_act_table_set("natural_log_exp_and_others")

            def x_hi(part):
                blocks = slice(XB * part, XB * (part + 1))
                for k in range(2):
                    act.wait_ge(x_in[2 * part + k], 16)
                    nc.scalar.activation(xh[k][:, blocks, :], xs[k][:, blocks, :], ACT.Copy).then_inc(x_high, 1)

            def hi(it, c):
                n = CHUNKS * it + c
                act.wait_ge(chunk_turned, n + 1)
                wait(act, chunk_multiplied, n - 1)
                nc.scalar.activation(ah[c % 2][:, :], at[c % 2][:, :, :].rearrange("p m t -> p (m t)"), ACT.Copy)\
                    .then_inc(chunk_high, 1)

            def first(it):
                for k in range(2):
                    act.wait_ge(ax_summed[k], it + 1)
                    nc.scalar.activation(hid[k][0][:, :], acc[k][:, :], ACT.Identity, scale=eps_sb[:, k:k + 1])\
                        .then_inc(layer_in[k], 1)

            def layer(it, l):
                for k in range(2):
                    act.wait_ge(layer_product, 2 * (LAYERS * it + l) + k + 1)
                    nc.scalar.activation(hid[k][l + 1][:, :], lay[k][:, :], ACT.Relu, bias=bias_sb[:, k, l:l + 1])\
                        .then_inc(layer_out, 1)

            def stage_a(it, mlp):
                for c in range(CHUNKS):
                    hi(it, c)
                    if not mlp and c in (0, 2, 4):
                        x_hi(c // 2 + 1)
                    after = it + (c + NROWS) // CHUNKS
                    load_rows(act, (2, 3), 0 if isinstance(after, int) and after == TILES else after, (c + NROWS) % CHUNKS)
                    if mlp and c == 0:
                        first(it - 1)
                    if mlp and c in (2, 3, 4):
                        layer(it - 1, c - 2)

            x_hi(0)
            stage_a(0, False)
            act.wait_ge(weights_in, 16 * WLOADS)
            nc.scalar.activation(eps_sb[:, :], eps_sb[:, :], ACT.Identity, bias=2.0).then_inc(small_prep, 1)
            act.wait_ge(small_prep, 1)
            act.wait_ge(w_in_turned, H)
            act.wait_ge(weights_turned, 8)
            for h in range(H):
                for k in range(TAPS):
                    nc.scalar.activation(w_nat[:, TAPS * h + k, :], bank[7][:, P * h:P * h + P], ACT.Copy,
                                         scale=conv_w_sb[:, h, k:k + 1]).then_inc(w_in_tapped, 1)
            with act.Fori(1, TILES - 1) as it:
                stage_a(it, True)
            stage_a(TILES - 1, True)
            first(TILES - 1)
            for l in range(LAYERS):
                layer(TILES - 1, l)

            act.preload_act_table_set("natural_log_exp_and_others")
            nc.scalar.activation(A_sb[:, :, :], A_sb[:, :, :], ACT.Exp).then_inc(small_prep, 1)
            act.wait_ge(small_prep, 2)
            nc.scalar.activation(A_sb[:, :, :], A_sb[:, :, :], ACT.Copy, scale=-1.0).then_inc(small_prep, 1)
            act.wait_ge(small_prep, 3)
            act.wait_ge(zeroed, 2)
            act.wait_ge(chunk_multiplied, TILES * CHUNKS)
            act.wait_ge(consts_set, 9)
            for at_ in (0, 4 * S):
                for blk in (slice(at_, at_ + 32), slice(at_ + 32, at_ + 64)):
                    nc.scalar.activation(sel[blk, :], ident[blk, at_:at_ + 32], ACT.Copy).then_inc(selectors_ready, 1)
            nc.scalar.activation(w_dth[:, :], w_dt_sb[:, :], ACT.Copy).then_inc(w_dt_parts, 1)

            def front_ax(a):
                act.wait_ge(ax1_summed, a + 1)
                wait(act, gcn_product, a)
                nc.scalar.activation(axT[:, :], accB[:, :], ACT.Copy).then_inc(ax1_ready, 1)

            def front_relu(a):
                act.wait_ge(gcn_product, a + 1)
                wait(act, f_normed, RG * a)
                nc.scalar.activation(g[:, :, :], M0g, ACT.Relu).then_inc(gcn_relu, 1)

            def front_hn(a):
                act.wait_ge(f_mean_negated, a + 1)
                wait(act, h_turned, a)
                for q in range(RG):
                    nc.scalar.activation(hn[:, q, :], g[:, q, :], ACT.Identity, bias=nb[:, q:q + 1],
                                         scale=rs[:, q:q + 1]).then_inc(f_normed, 1)

            def front_hT(a):
                act.wait_ge(h_turned, a + 1)
                wait(act, z_product, H * a)
                nc.scalar.activation(hT[:, 0:TAPS - 1], hT[:, TILE:TILE + TAPS - 1], ACT.Copy).then_inc(history_kept, 1)
                act.wait_ge(history_kept, a + 1)
                nc.scalar.activation(hT[:, TAPS - 1:], M1[:, :], ACT.Identity, bias=ln_b_sb[:, :], scale=ln_g_sb[:, :])\
                    .then_inc(h_ready, 1)

            def front_silu(a, par):
                wait(act, y_skipped, a - 1)
                wait(act, y_gated, a - 1)
                for h, m in enumerate((M0, M1)):
                    act.wait_ge(conv_summed, H * a + h + 1)
                    nc.scalar.activation(u[par][:, h, :], m[:, :], ACT.Silu, bias=conv_b_sb[:, h:h + 1]).then_inc(u_ready, 1)
                for h, m in enumerate((M0, M1)):
                    act.wait_ge(z_product, H * a + h + 1)
                    nc.scalar.activation(sz[par][:, h, :], m[:, :], ACT.Silu).then_inc(gate_ready, 1)
                act.preload_act_table_set("natural_log_exp_and_others")

            def front_bc(a, par):
                act.wait_ge(bcdt_product, a + 1)
                wait(act, C_spread, S * (a - 1))
                nc.scalar.activation(bc[par][:, :], M0[:, :], ACT.Copy).then_inc(bcdt_high, 1)

            def front_sp(a, par, step):
                if step == 0:
                    act.wait_ge(dt_product, H * (a + 1))
                    wait(act, dt_ready, a)
                    for h, m in enumerate((M1, M0)):
                        nc.scalar.activation(sp_a[:, h, :], m[:, :], ACT.Abs, bias=b_dt_sb[:, h:h + 1]).then_inc(sp_abs_relu, 1)
                        nc.scalar.activation(sp_r[:, h, :], m[:, :], ACT.Relu, bias=b_dt_sb[:, h:h + 1]).then_inc(sp_abs_relu, 1)
                else:
                    act.wait_ge(sp_abs_relu, 4 * a + 4)
                    nc.scalar.activation(sp_a[:, :, :], sp_a[:, :, :], ACT.Exp, scale=-1.0).then_inc(sp_exp, 1)
                    act.wait_ge(sp_exp, a + 1)
                    nc.scalar.activation(dtu[par][:, :, :], sp_a[:, :, :], ACT.Identity, bias=1.0).then_inc(sp_one_plus, 1)
                    act.wait_ge(sp_one_plus, a + 1)
                    nc.scalar.activation(dt_[par][:, :, :], dtu[par][:, :, :], ACT.Ln).then_inc(sp_log, 1)

            def window(b, par, tail, front):
                for n in range(S + (0 if front else LAG)):
                    k = n - LAG
                    if k >= 0 or tail:
                        act.wait_ge(scanned, S * b + k + 1)
                        nc.scalar.activation(state[:, k % S, :], hs[k % NHS][:, :, TILE], ACT.Copy)\
                            .then_inc(state_kept, 1)
                    if n < S:
                        if n == 0:
                            act.wait_ge(dt_ready, b + 1)
                        wait(act, scanned, S * b + n - NDA + 1)
                        for h in range(H):
                            nc.scalar.activation(dA[n % NDA][:, h, 1:], dt_[par][:, h, :], ACT.Exp,
                                                 scale=A_sb[:, h, n:n + 1]).then_inc(dA_ready, 1)
                    first = n - AT['act_start']
                    for k in range(first, S if n == S - 1 else min(first + 1, S - 1)):
                        if not 0 <= k < S:
                            continue
                        same = [j for j in range(-S, k) if (j % S in POOL_B) == (k in POOL_B)]
                        wait(act, scanned, S * b + same[-2] + 1)
                        wait(act, state_kept, S * (b - 1) + k + 1)
                        nc.scalar.activation(dBu(k, par)[:, :, 0], state[:, k, :], ACT.Copy).then_inc(start_set, 1)
                    k = n - AT['act_B']
                    if k in POOL_B:
                        act.wait_ge(B_spread, S * b + k + 1)
                        wait(act, dBu_by_pool, NPB * b + nB(k) - 1)
                        nc.scalar.activation(b_sb[(nB(k) + NPB * par) % 2][:, :], BB[k % 2][:, :], ACT.Copy).then_inc(B_copied, 1)
                    if front:
                        if n == 0:
                            front_ax(b + 1)
                        if n == AT['act_g']:
                            front_relu(b + 1)
                        if n == AT['act_hn']:
                            front_hn(b + 1)
                        if n == AT['act_hT']:
                            front_hT(b + 1)
                        if n == AT['act_silu']:
                            front_silu(b + 1, 1 - par)
                        if n == AT['act_bc']:
                            front_bc(b + 1, 1 - par)
                        if n == AT['act_sp']:
                            front_sp(b + 1, 1 - par, 0)
                        if n == AT['act_exp']:
                            front_sp(b + 1, 1 - par, 1)
                    if tail and n == AT['act_tail']:
                        tail_norm(b - 1)

            def tail_norm(b):
                act.wait_ge(o_mean_negated, b + 1)
                wait(act, out_stored, 16 * b)
                for q in range(RG):
                    nc.scalar.activation(o_n[:, q, :], O[:, q, :], ACT.Identity, bias=nb2[:, q:q + 1],
                                         scale=rs2[:, q:q + 1]).then_inc(o_normed, 1)

            front_ax(0)
            front_relu(0)
            front_hn(0)
            front_hT(0)
            stage_a_over(act)
            front_silu(0, 0)
            front_bc(0, 0)
            front_sp(0, 0, 0)
            front_sp(0, 0, 1)
            window(0, 0, False, True)
            window(1, 1, True, True)
            with act.Fori(0, 2) as i:
                window(2 * i + 2, 0, True, True)
                window(2 * i + 3, 1, True, True)
            window(6, 0, True, True)
            window(7, 1, True, False)
            tail_norm(TILES - 1)

        @block.vector
        def _(dve):
            def x_lo(part):
                blocks = slice(XB * part, XB * (part + 1))
                for k in range(2):
                    dve.wait_ge(x_high, 2 * part + k + 1)
                    nc.vector.tensor_tensor(xl[k][:, blocks, :], xs[k][:, blocks, :], xh[k][:, blocks, :], ALU.subtract)\
                        .then_inc(x_low, 1)

            def transpose(it, c):
                n = CHUNKS * it + c
                dve.wait_ge(rows_in[c % NROWS], 16 * Q * (CHUNKS // NROWS * it + c // NROWS + 1))
                if isinstance(it, int) and it == TILES and c >= 2:
                    dve.wait_ge(chunk_multiplied, n - 1)
                else:
                    wait(dve, chunk_low, n - 1)
                    if not (isinstance(it, int) and it == 0):
                        dve.wait_ge(chunk_stored[c % 2], 16 * (CHUNKS // 2 * (it - 1) + c // 2 + 1))
                half = GROUPS // 2
                for j in range(2):
                    src = rows[c % NROWS][:, half * j:half * j + half, :]
                    dst = at[c % 2][:, :, 32 * half * j:32 * half * (j + 1)]
                    last = nc.vector.transpose(dst.rearrange("p m (g i) -> p g m i", i=32),
                                               src.rearrange("p g (i m) -> p g m i", i=32))
                last.then_inc(chunk_turned, 1)

            def lo(it, c):
                n = CHUNKS * it + c
                dve.wait_ge(chunk_high, n + 1)
                wait(dve, chunk_multiplied, n - 1)
                nc.vector.tensor_tensor(al[c % 2][:, :], at[c % 2][:, :, :].rearrange("p m t -> p (m t)"),
                                        ah[c % 2][:, :], ALU.subtract).then_inc(chunk_low, 1)

            def norm_stats(it):
                dve.wait_ge(stacks_merged, it + 1)
                nc.vector.tensor_tensor(ysum[:, :, :], mrg, bm_sb[:, :].unsqueeze(1).to_broadcast([P, RG, D]), ALU.add)\
                    .then_inc(bm_added, 1)
                dve.wait_ge(bm_added, it + 1)
                dve.wait_ge(x_tile_in, 16 * it + 16)
                nc.vector.tensor_tensor(ysum[:, :, :], ysum[:, :, :], res[0][:, :, :], ALU.add).then_inc(x_added, 1)
                dve.wait_ge(x_added, it + 1)
                for q in range(RG):
                    last = nc.vector.bn_stats(stats[:, q, :], ysum[:, q, :])
                last.then_inc(a_stats, 1)
                dve.wait_ge(a_stats, it + 1)
                nc.vector.tensor_copy(stat_in[:, :], stats[:, 0, 0:1])
                for q in range(RG):
                    last = nc.vector.bn_aggr(mv[:, q, :], stats[:, q, :])
                last.then_inc(a_mean_var, 1)

            def norm_apply(it):
                dve.wait_ge(a_inv_dev, it + 1)
                for q in range(RG):
                    last = nc.vector.tensor_scalar(xn[:, q, :], ysum[:, q, :], mv[:, q, 0:1], rs[:, q:q + 1],
                                                   ALU.subtract, ALU.mult)
                last.then_inc(x1_normed, 1)

            def stage_a(it, mlp):
                for c in range(CHUNKS):
                    transpose(it, c)
                    if not mlp and c == 0:
                        x_lo(0)
                    if c > 0:
                        lo(it, c - 1)
                    elif mlp:
                        lo(it - 1, CHUNKS - 1)
                    if not mlp and c % 2 and c < CHUNKS - 1:
                        x_lo((c + 1) // 2)
                    if mlp and c == 6:
                        norm_stats(it - 1)
                    if mlp and c == 7:
                        norm_apply(it - 1)

            stage_a(0, False)
            for k in range(2):
                dve.wait_ge(weights_turned, 4 * (k + 1))
                nc.vector.tensor_copy(w_T[:, 4 * k:4 * k + 4, :].rearrange("p a b -> p (a b)"), bank[5 + k][:, :])\
                    .then_inc(weights_T_ready, 1)
            with dve.Fori(1, TILES) as it:
                stage_a(it, True)
            transpose(TILES, 0)
            lo(TILES - 1, CHUNKS - 1)
            transpose(TILES, 1)
            for h in range(H):
                dve.wait_ge(w_taps_turned, TAPS * (h + 1))
                nc.vector.tensor_copy(w_cv_sb[:, h, :, :].rearrange("p a b -> p (a b)"), bank[5 + h][:, :]).then_inc(w_taps_ready, 1)
            transpose(TILES, 2)
            norm_stats(TILES - 1)
            norm_apply(TILES - 1)
            for c in range(3, CHUNKS):
                transpose(TILES, c)

            dve.wait_ge(x1_normed, TILES)
            dve.sem_inc(engines_through, 1)
            dve.wait_ge(zeroed, 2)

            def front_g(a):
                dve.wait_ge(gcn_relu, a + 1)
                for q in range(RG):
                    last = nc.vector.bn_stats(stats[:, q, :], g[:, q, :])
                last.then_inc(f_stats, 1)
                dve.wait_ge(f_stats, a + 1)
                nc.vector.tensor_copy(stat_in[:, :], stats[:, 0, 0:1])
                for q in range(RG):
                    last = nc.vector.bn_aggr(mv[:, q, :], stats[:, q, :])
                last.then_inc(f_mean_var, 1)

            def front_bclo(a, par):
                dve.wait_ge(bcdt_high, a + 1)
                low = slice(4 * S, P)
                nc.vector.tensor_tensor(bc[par][low, :], M0[low, :], bc[par][low, :], ALU.subtract).then_inc(bcdt_low, 1)

            def front_spd(a, par):
                dve.wait_ge(sp_log, a + 1)
                nc.vector.scalar_tensor_tensor(sp_a[:, :, :], dtu[par][:, :, :], -1.0, sp_a[:, :, :], ALU.add, ALU.subtract)\
                    .then_inc(sp_error, 1)

            def tail_y(b, par):
                dve.wait_ge(y_added, (S - 1) * (b + 1))
                for h in range(H):
                    last = nc.vector.scalar_tensor_tensor(y[par][:, h, :], u[par][:, h, :], D_sb[:, h:h + 1], y[par][:, h, :],
                                                          ALU.mult, ALU.add)
                last.then_inc(y_skipped, 1)

            def tail_stats(b, par):
                dve.wait_ge(projected, b + 1)
                for q in range(RG):
                    last = nc.vector.bn_stats(stats2[:, q, :], O[:, q, :])
                last.then_inc(o_stats, 1)
                dve.wait_ge(o_stats, b + 1)
                nc.vector.tensor_copy(stat_in[:, :], stats2[:, 0, 0:1])
                for q in range(RG):
                    last = nc.vector.bn_aggr(mv2[:, q, :], stats2[:, q, :])
                last.then_inc(o_mean_var, 1)

            def window(b, par, tail, front):
                for n in range(S + 2):
                    if n < S and n not in POOL_B:
                        dve.wait_ge(B_spread, S * b + n + 1)
                        if n == 0:
                            dve.wait_ge(dtu_ready, b + 1)
                        wait(dve, scanned, S * b + n - 1)
                        nc.vector.tensor_tensor(dBuV[dve_slot(n, par)][:, :, 1:], dtu[par][:, :, :],
                                                BB[n % 2][:, :].unsqueeze(1).to_broadcast([P, H, TILE]), ALU.mult)\
                            .then_inc(dBu_by_dve, 1)
                    k = n - 1
                    if 0 <= k < S:
                        dve.wait_ge(dA_ready, H * (S * b + k + 1))
                        if k in POOL_B:
                            dve.wait_ge(dBu_by_pool, NPB * b + nB(k) + 1)
                        else:
                            dve.wait_ge(dBu_by_dve, NVB * b + k - nB(k) + 1)
                        wait(dve, state_kept, S * b + k - NHS + 1)
                        wait(dve, C_multiplied, S * b + k - NHS + 1)
                        dve.wait_ge(start_set, S * b + k + 1)
                        flat = [a[:, :, :].rearrange("p h t -> p (h t)") for a in (hs[k % NHS], dA[k % NDA], dBu(k, par))]
                        nc.vector.tensor_tensor_scan(flat[0], flat[1], flat[2], zero[:, :], ALU.mult, ALU.add)\
                            .then_inc(scanned, 1)
                    k = n - 2
                    if k >= 0:
                        dve.wait_ge(C_spread, S * b + k + 1)
                        dve.wait_ge(scanned, S * b + k + 1)
                        wait(dve, y_added, (S - 1) * b + (max(k - NPR, 1) if k >= NPR else k - NPR + 1))
                        nc.vector.tensor_tensor(pr[k % NPR][:, :, :], hs[k % NHS][:, :, 1:],
                                                CC[k % 2][:, :].unsqueeze(1).to_broadcast([P, H, TILE]), ALU.mult)\
                            .then_inc(C_multiplied, 1)
                    if front:
                        if n == AT['dve_g']:
                            front_g(b + 1)
                        if n == AT['dve_bc']:
                            front_bclo(b + 1, 1 - par)
                        if n == AT['dve_sp']:
                            front_spd(b + 1, 1 - par)
                    if tail:
                        if n == AT['dve_y']:
                            tail_y(b - 1, 1 - par)
                        if n == AT['dve_tail']:
                            tail_stats(b - 1, 1 - par)

            dve.wait_ge(w_dt_parts, 1)
            nc.vector.tensor_tensor(w_dtl[:, :], w_dt_sb[:, :], w_dth[:, :], ALU.subtract).then_inc(w_dt_parts, 1)
            front_g(0)
            stage_a_over(dve)
            front_bclo(0, 0)
            front_spd(0, 0)
            dve.wait_ge(sp_error, 1)
            nc.vector.tensor_tensor(dt_[0][:, :, :], dt_[0][:, :, :], sp_a[:, :, :], ALU.subtract).then_inc(sp_corrected, 1)
            dve.wait_ge(sp_corrected, 1)
            nc.vector.tensor_tensor(dt_[0][:, :, :], dt_[0][:, :, :], sp_r[:, :, :], ALU.add).then_inc(dt_ready, 1)
            dve.wait_ge(dt_ready, 1)
            nc.vector.tensor_tensor(dtu[0][:, :, :], dt_[0][:, :, :], u[0][:, :, :], ALU.mult).then_inc(dtu_ready, 1)
            dve.wait_ge(zeroed, 2 + NDA)
            window(0, 0, False, True)
            window(1, 1, True, True)
            with dve.Fori(0, 2) as i:
                window(2 * i + 2, 0, True, True)
                window(2 * i + 3, 1, True, True)
            window(6, 0, True, True)
            window(7, 1, True, False)
            tail_y(TILES - 1, 1)
            dve.wait_ge(y_skipped, TILES)
            nc.vector.tensor_tensor(y[1][:, :, :], y[1][:, :, :], sz[1][:, :, :], ALU.mult).then_inc(y_gated, 1)
            tail_stats(TILES - 1, 1)

        @block.tensor
        def _(pe):
            mm = nc.tensor.matmul
            def chunk(it, c):
                n = CHUNKS * it + c
                pe.wait_ge(chunk_low, n + 1)
                for k in range(2):
                    if c == 0:
                        wait(pe, layer_in[k], it)
                    if isinstance(it, int) and it == 0 and CH * c % XB == 0:
                        pe.wait_ge(x_low, 2 * (CH * c // XB) + k + 1)
                    for m in range(CH):
                        b = CH * c + m
                        cols = slice(m * TILE, (m + 1) * TILE)
                        for j, (w, v) in enumerate(((xh[k], ah), (xl[k], ah), (xh[k], al))):
                            last = mm(acc[k][:, :], w[:, b, :], v[c % 2][:, cols], start=(b == 0 and j == 0),
                                      stop=(b == KB - 1 and j == 2))
                    if c == CHUNKS - 1:
                        last.then_inc(ax_summed[k], 1)
                        if k == 1:
                            pe.wait_ge(ax_summed[1], it + 1)
                            pe.sem_inc(chunk_multiplied, 1)
                    elif k == 1:
                        last.then_inc(chunk_multiplied, 1)

            def layer(it, l):
                for k in range(2):
                    if l == 0:
                        pe.wait_ge(layer_in[k], it + 1)
                        pe.wait_ge(weights_T_ready, 2)
                    else:
                        pe.wait_ge(layer_out, 2 * (LAYERS * it + l - 1) + k + 1)
                    mm(lay[k][:, :], w_T[:, LAYERS * k + l, :], hid[k][l][:, :], start=True, stop=True).then_inc(layer_product, 1)

            def merge(it):
                pe.wait_ge(layer_out, 2 * LAYERS * (it + 1))
                for q in range(RG):
                    for k in range(2):
                        last = mm(mrg[:, q, :], hid[k][LAYERS][:, P * q:P * q + P], w_T[:, 2 * LAYERS + k, :],
                                  start=(k == 0), stop=(k == 1))
                last.then_inc(stacks_merged, 1)

            def weights():
                pe.wait_ge(weights_in, 16 * WLOADS)
                pe.wait_ge(consts_set, 4)
                for j in range(2 * LAYERS + 2):
                    nc.tensor.transpose(bank[5 + j // 4][:, D * (j % 4):D * (j % 4) + D], w_nat[:, j, :], ident[:, :])\
                        .then_inc(weights_turned, 1)
                for h in range(H):
                    nc.tensor.transpose(bank[7][:, P * h:P * h + P], w_in_sb[:, P * h:P * h + P], ident[:, :]).then_inc(w_in_turned, 1)

            def stage_a(it, mlp):
                for c in range(CHUNKS):
                    chunk(it, c)
                    if mlp and c < LAYERS:
                        layer(it - 1, c)
                    if mlp and c == LAYERS:
                        merge(it - 1)
                    if not mlp and c == CHUNKS - 3:
                        weights()

            stage_a(0, False)
            with pe.Fori(1, TILES) as it:
                stage_a(it, True)
            pe.wait_ge(w_in_tapped, H * TAPS)
            pe.wait_ge(weights_T_ready, 2)
            for h in range(H):
                for k in range(TAPS):
                    nc.tensor.transpose(bank[5 + h][:, P * k:P * k + P], w_nat[:, TAPS * h + k, :], ident[:, :])\
                        .then_inc(w_taps_turned, 1)
            def adj_tile0(blocks):
                for b in blocks:
                    c, m = b // CH, b % CH
                    if m == 0:
                        pe.wait_ge(chunk_turned, CHUNKS * TILES + c + 1)
                        pe.wait_ge(x1_in, 16 * (c + 1))
                    last = mm(accB[:, :], xm[:, b, :], at[c % 2][:, m, :], start=(b == 0), stop=(b == KB - 1))
                    if b == KB - 1:
                        last.then_inc(ax1_summed, 1)
                    elif m == CH - 1:
                        last.then_inc(chunk_multiplied, 1)

            adj_tile0(range(1))
            for l in range(LAYERS):
                layer(TILES - 1, l)
                adj_tile0(range(l + 1, l + 2))
            merge(TILES - 1)
            adj_tile0(range(LAYERS + 1, KB))


            def adj_blocks(a, b0, b1):
                for b in range(b0, b1):
                    c, m = b // CH, b % CH
                    if m == 0:
                        pe.wait_ge(adjT_in[c % NADJ], 16 * (CHUNKS // NADJ * (a - 1) + c // NADJ + 1))
                    if b == 0:
                        wait(pe, ax1_ready, a)
                    last = mm(accB[:, :], xm[:, b, :], adjc[c % NADJ][:, m, :], start=(b == 0), stop=(b == KB - 1))
                    if b == KB - 1:
                        last.then_inc(ax1_summed, 1)
                        pe.wait_ge(ax1_summed, a + 1)
                        pe.sem_inc(adjT_multiplied, 1)
                    elif m == CH - 1:
                        last.then_inc(adjT_multiplied, 1)

            def front_gcn(a):
                pe.wait_ge(ax1_ready, a + 1)
                wait(pe, sp_abs_relu, 4 * a)
                for q in range(RG):
                    mm(M0g[:, q, :], axT[:, P * q:P * q + P], gcn_w_sb[:, :], start=True, stop=False)
                    last = mm(M0g[:, q, :], ones[0:1, :], gcn_b_sb[0:1, :], start=False, stop=True)
                last.then_inc(gcn_product, 1)

            def front_tr(a):
                pe.wait_ge(f_normed, RG * (a + 1))
                for q in range(RG):
                    last = nc.tensor.transpose(M1[:, P * q:P * q + P], hn[:, q, :], ident[:, :])
                last.then_inc(h_turned, 1)

            def front_xc(a, j0, j1):
                for j in range(j0, j1):
                    h, k = j // TAPS, j % TAPS
                    if j == 0:
                        pe.wait_ge(h_ready, a + 1)
                        pe.wait_ge(gcn_relu, a + 1)
                    last = mm((M0, M1)[h][:, :], w_cv_sb[:, h, k, :], hT[:, k:k + TILE], start=(k == 0), stop=(k == TAPS - 1))
                    if k == TAPS - 1:
                        last.then_inc(conv_summed, 1)

            def front_z(a, h):
                m = (M0, M1)[h]
                pe.wait_ge(u_ready, H * a + h + 1)
                mm(m[:, :], w_in_sb[:, DI + P * h:DI + P * h + P], hT[:, TAPS - 1:], start=True, stop=True).then_inc(z_product, 1)

            def front_dbc(a, par):
                pe.wait_ge(gate_ready, 2 * a + 2)
                pe.wait_ge(u_ready, H * (a + 1))
                for h in range(H):
                    last = mm(M0[:, :], w_xp_sb[:, h, :], u[par][:, h, :], start=(h == 0), stop=(h == 1))
                last.then_inc(bcdt_product, 1)

            def front_dtp(a, par):
                pe.wait_ge(bcdt_low, a + 1)
                for h, m in enumerate((M1, M0)):
                    mm(m[:, :], w_dth[:, P * h:P * h + P], bc[par][:, :], start=True, stop=False)
                    mm(m[:, :], w_dtl[:, P * h:P * h + P], bc[par][:, :], start=False, stop=True).then_inc(dt_product, 1)

            def spread_B(b, n, par):
                if n == 0:
                    pe.wait_ge(bcdt_low, b + 1)
                k, bb = (n - 2, b) if n >= 2 else (n - 2 + S, b - 1)
                if not (isinstance(bb, int) and bb < 0):
                    if k in POOL_B:
                        pe.wait_ge(B_copied, NPB * bb + nB(k) + 1)
                    else:
                        pe.wait_ge(dBu_by_dve, NVB * bb + k - nB(k) + 1)
                mm(BB[n % 2][:, :], sel[:, n:n + 1].to_broadcast([P, P]), bc[par][:, :], start=True, stop=True).then_inc(B_spread, 1)

            def spread_C(b, n, par):
                wait(pe, C_multiplied, S * b + n - 1)
                mm(CC[n % 2][:, :], sel[:, S + n:S + n + 1].to_broadcast([P, P]), bc[par][:, :], start=True, stop=True).then_inc(C_spread, 1)

            def tail_out(b, par, groups):
                if groups[0] == 0:
                    pe.wait_ge(y_gated, b + 1)
                    wait(pe, o_normed, RG * b)
                    pe.wait_ge(x1_tile_in[par], 8 * (b - par) + 16)
                for q in groups:
                    mm(O[:, q, :], ident[:, :], res[par][:, q, :], start=True, stop=False)
                    for h in range(H):
                        last = mm(O[:, q, :], y[par][:, h, P * q:P * q + P], w_out_sb[:, h, :], start=False, stop=(h == 1))
                if groups[-1] == RG - 1:
                    last.then_inc(projected, 1)


            def first_spreads(b, par):
                spread_B(b, 0, par)
                spread_B(b, 1, par)
                spread_C(b, 0, par)

            def window(b, par, tail, front, adj_):
                if tail or not front:
                    first_spreads(b, par)
                for n in range(S):
                    if n > 0:
                        spread_C(b, n, par)
                    if n + 2 < S:
                        spread_B(b, n + 2, par)
                    if front:
                        if n == 0:
                            front_gcn(b + 1)
                        if n == AT['pe_tr']:
                            front_tr(b + 1)
                        front_xc(b + 1, sum(CONV[:n]), sum(CONV[:n + 1]))
                        if n == AT['pe_z']:
                            front_z(b + 1, 0)
                            front_z(b + 1, 1)
                        if n == AT['pe_dbc']:
                            front_dbc(b + 1, 1 - par)
                        if n == AT['pe_dt']:
                            front_dtp(b + 1, 1 - par)
                    if tail and 0 <= n - AT['pe_out'] < 2:
                        half = RG // 2 * (n - AT['pe_out'])
                        tail_out(b - 1, 1 - par, range(half, half + RG // 2))
                    if adj_:
                        adj_blocks(b + 2, sum(PLAN[:n]), sum(PLAN[:n + 1]))

            pe.wait_ge(w_taps_ready, H)
            pe.wait_ge(w_dt_parts, 2)
            def fill(k):
                adj_blocks(1, sum(FILL[:k]), sum(FILL[:k + 1]))

            fill(0)
            front_gcn(0)
            fill(1)
            front_tr(0)
            fill(2)
            front_xc(0, 0, TAPS)
            fill(3)
            front_xc(0, TAPS, H * TAPS)
            fill(4)
            front_z(0, 0)
            front_z(0, 1)
            fill(5)
            front_dbc(0, 0)
            fill(6)
            front_dtp(0, 0)
            fill(7)
            pe.wait_ge(selectors_ready, 4)
            first_spreads(0, 0)
            fill(8)
            window(0, 0, False, True, True)
            window(1, 1, True, True, True)
            with pe.Fori(0, 2) as i:
                window(2 * i + 2, 0, True, True, True)
                window(2 * i + 3, 1, True, True, True)
            window(6, 0, True, True, False)
            window(7, 1, True, False, False)
            tail_out(TILES - 1, 1, range(RG))


_INS = ['x', 'adj', 'L0_gnn_x2', 'L0_gnn_eps1', 'L0_gnn_eps2', 'L0_gnn_W1', 'L0_gnn_b1', 'L0_gnn_W2', 'L0_gnn_b2',
        'L0_gnn_Wm', 'L0_gnn_bm', 'L1_gnn_gcn_w', 'L1_gnn_gcn_b', 'L1_gnn_ln_g', 'L1_gnn_ln_b', 'L1_gnn_w_in',
        'L1_gnn_conv_w', 'L1_gnn_conv_b', 'L1_gnn_w_xp', 'L1_gnn_w_dt', 'L1_gnn_b_dt', 'L1_gnn_A_log',
        'L1_gnn_D_skip', 'L1_gnn_w_out']


def kernel(**inputs):
    import numpy as np
    import concourse.bacc as bacc
    from concourse import mybir as _mybir
    from concourse.bass_utils import run_bass_kernel_spmd

    nc = bacc.Bacc("TRN2", target_bir_lowering=False, num_devices=1)
    arrays, args = {}, []
    for name in _INS:
        a = np.ascontiguousarray(inputs[name])
        arrays[f"in_{name}"] = a
        args.append(nc.dram_tensor(f"in_{name}", a.shape, _mybir.dt.from_np(a.dtype), kind="ExternalInput").ap())
    out = nc.dram_tensor("out", (4096, 128), _mybir.dt.float32, kind="ExternalOutput").ap()
    gnn_mamba(nc, *args, out)
    r = run_bass_kernel_spmd(nc, [arrays], core_ids=[0])
    return r.results[0]["out"]
```
